# Optimizing a Trainium2 kernel written in Bass

```python
import numpy as np
import jax
import jax.numpy as jnp

def _softmax(x, axis=-1):
    return jax.nn.softmax(x, axis=axis)

def _gelu(x):
    return jax.nn.gelu(x, approximate=True)

def _silu(x):
    return jax.nn.silu(x)

def _sigmoid(x):
    return jax.nn.sigmoid(x)

def _layernorm(x, axis=-1, eps=1e-05):
    m = jnp.mean(x, axis=axis, keepdims=True)
    v = jnp.var(x, axis=axis, keepdims=True)
    return (x - m) / jnp.sqrt(v + eps)

def _scatter_add(tgt, idx, src, axis=0):
    return tgt.at[idx].add(src)

def _segment_sum(src, seg, n):
    return jax.ops.segment_sum(src, seg, n)
kernel_name = 'mk_adj_preln_d2_adj_r2_198e9d'

def setup_inputs(seed: int=0):
    np.random.seed(seed)
    _w = jnp.asarray

    def _rec_inputs():
        import jax
        import jax.numpy as jnp
        _gk = jax.random.key(seed)
        x = -0.0005207 + 1.001 * jax.random.normal(jax.random.fold_in(_gk, 1), (4096, 128), jnp.float32)
        _a = jax.random.bernoulli(jax.random.fold_in(_gk, 2), 0.000976562, (4096, 4096))
        adj = _a.astype(jnp.int32)
        return (x, adj)
    x, adj = _rec_inputs()

    def _L0_gnn_setup():
        import jax, jax.numpy as jnp
        import numpy as np
        N, IN_DIM, OUT_DIM = (4096, 128, 128)
        NEG_INF = -1000000000.0
        key = jax.random.key(seed)
        k1, k2, k3, k4 = jax.random.split(key, 4)
        X = jax.random.normal(k1, (N, IN_DIM), dtype=jnp.float32)
        A = jax.random.randint(k2, (N, N), 0, 2).astype(jnp.int32)
        W_fc = jax.random.normal(k3, (IN_DIM, OUT_DIM), dtype=jnp.float32) * (1.0 / np.sqrt(IN_DIM))
        b_fc = jnp.zeros((OUT_DIM,), dtype=jnp.float32)
        w_att = jax.random.normal(k4, (2 * OUT_DIM,), dtype=jnp.float32) * (1.0 / np.sqrt(2 * OUT_DIM))
        b_att = jnp.zeros((), dtype=jnp.float32)
        return {'X': X, 'A': A, 'W_fc': W_fc, 'b_fc': b_fc, 'w_att': w_att, 'b_att': b_att}
    _L0_gnn_all = _L0_gnn_setup()
    _L0_gnn_in = {k: v for k, v in _L0_gnn_all.items() if k in ('W_fc', 'b_fc', 'w_att', 'b_att')}
    del _L0_gnn_all

    def _L1_gnn_setup():
        import jax, jax.numpy as jnp
        import numpy as np
        NUM_HEADS = 4
        ALPHA = 0.2
        NEG_INF = -9000000000000000.0
        LN_EPS = 1e-05
        key = jax.random.key(seed)
        k_x, k_adj, k_W, k_a, k_g, k_b = jax.random.split(key, 6)
        N, Fin, Fout = (2048, 128, 128)
        head_dim = Fout // NUM_HEADS
        x = jax.random.normal(k_x, (N, Fin), dtype=jnp.float32)
        adj = jax.random.randint(k_adj, (N, N), 0, 2, dtype=jnp.int32)
        lim_W = 1.414 * np.sqrt(6.0 / (Fin + Fout))
        W = jax.random.uniform(k_W, (Fin, Fout), jnp.float32, -lim_W, lim_W)
        lim_a = 1.414 * np.sqrt(6.0 / (2 * head_dim + 1))
        a = jax.random.uniform(k_a, (2 * head_dim, 1), jnp.float32, -lim_a, lim_a)
        gamma = jax.random.normal(k_g, (Fout,), dtype=jnp.float32) * 0.1 + 1.0
        beta = jax.random.normal(k_b, (Fout,), dtype=jnp.float32) * 0.1
        return {'x': x, 'adj': adj, 'W': W, 'a': a, 'gamma': gamma, 'beta': beta}
    _L1_gnn_all = _L1_gnn_setup()
    _L1_gnn_in = {k: v for k, v in _L1_gnn_all.items() if k in ('W', 'a', 'gamma', 'beta')}
    del _L1_gnn_all
    return {'x': x, 'adj': adj, 'L0_gnn_W_fc': _L0_gnn_in['W_fc'], 'L0_gnn_b_fc': _L0_gnn_in['b_fc'], 'L0_gnn_w_att': _L0_gnn_in['w_att'], 'L0_gnn_b_att': _L0_gnn_in['b_att'], 'L1_gnn_W': _L1_gnn_in['W'], 'L1_gnn_a': _L1_gnn_in['a'], 'L1_gnn_gamma': _L1_gnn_in['gamma'], 'L1_gnn_beta': _L1_gnn_in['beta']}

def reference(x, adj, L0_gnn_W_fc, L0_gnn_b_fc, L0_gnn_w_att, L0_gnn_b_att, L1_gnn_W, L1_gnn_a, L1_gnn_gamma, L1_gnn_beta):
    import jax
    import jax.numpy as jnp

    def _L0_gnn_ref(X, A, W_fc, b_fc, w_att, b_att):
        import jax, jax.numpy as jnp
        import numpy as np
        N, IN_DIM, OUT_DIM = (4096, 128, 128)
        NEG_INF = -1000000000.0
        H = X @ W_fc + b_fc
        d = H.shape[1]
        s_src = H @ w_att[:d]
        s_dst = H @ w_att[d:]
        scores = s_src[:, None] + s_dst[None, :] + b_att
        scores = jnp.where(A > 0, scores, jnp.float32(NEG_INF))
        alpha = jax.nn.softmax(scores, axis=1)
        return alpha @ H

    def _L1_gnn_ref(x, adj, W, a, gamma, beta):
        import jax, jax.numpy as jnp
        import numpy as np
        NUM_HEADS = 4
        ALPHA = 0.2
        NEG_INF = -9000000000000000.0
        LN_EPS = 1e-05
        N = x.shape[0]
        H = NUM_HEADS
        D = W.shape[1] // H
        h = (x @ W).reshape(N, H, D)
        a1, a2 = (a[:D, 0], a[D:, 0])
        si = jnp.einsum('nhd,d->nh', h, a1)
        sj = jnp.einsum('nhd,d->nh', h, a2)
        e = si[:, :, None] + sj.T[None, :, :]
        e = jnp.where(e > 0, e, ALPHA * e)
        mask = adj[:, None, :] > 0
        e = jnp.where(mask, e, NEG_INF)
        attn = jax.nn.softmax(e, axis=-1)
        out = jnp.einsum('nhm,mhd->nhd', attn, h).reshape(N, H * D)
        mu = out.mean(axis=-1, keepdims=True)
        var = out.var(axis=-1, keepdims=True)
        return gamma * (out - mu) * jax.lax.rsqrt(var + LN_EPS) + beta
    h = jnp.maximum(_layernorm(x, axis=-1), 0.0)
    x = x + _L0_gnn_ref(h, adj, L0_gnn_W_fc, L0_gnn_b_fc, L0_gnn_w_att, L0_gnn_b_att)
    h = jnp.maximum(_layernorm(x, axis=-1), 0.0)
    x = x + _L1_gnn_ref(h, adj, L1_gnn_W, L1_gnn_a, L1_gnn_gamma, L1_gnn_beta)
    return x

_drawn_inputs = setup_inputs


def setup_inputs(seed=0):
    import zlib

    import numpy as np

    out = dict(_drawn_inputs(seed))
    spreads = {'L0_gnn_b_fc': (0.0, 0.1)}
    factors = {}
    for name, (base, spread) in spreads.items():
        noise = np.random.default_rng([zlib.crc32(name.encode()), seed]).standard_normal(out[name].shape)
        drawn = base * np.exp(spread * noise) if base else spread * noise
        out[name] = jnp.asarray(drawn.astype(out[name].dtype))
    for name, factor in factors.items():
        out[name] = (out[name] * factor).astype(out[name].dtype)
    return out
```

```python
import numpy as np
from contextlib import ExitStack
import concourse.bass as bass
from concourse import mybir

ALU = mybir.AluOpType
ACT = mybir.ActivationFunctionType
X_AXIS = mybir.AxisListType.X
F32, BF16, FP8 = mybir.dt.float32, mybir.dt.bfloat16, mybir.dt.float8e4
I32, U32, I16, I8, U8 = mybir.dt.int32, mybir.dt.uint32, mybir.dt.int16, mybir.dt.int8, mybir.dt.uint8
ds = bass.ds

P = 128
N = 4096
T = N // P
D = 128
H = 4
HD = D // H
HW = HD + 1
ALPHA = 0.2
EPS = 1e-5
EXP_SHIFT = 60.0
ONE_FP8 = 0x38

W0 = D + 1
G_COLS = 3 * W0 + 1
QUARTERS = 4
QCOLS = T // QUARTERS * P

CHUNK_TILES = 8
CHUNKS = T // CHUNK_TILES
CH = CHUNK_TILES * P
UNITS = H * CHUNKS
GT = 4
GROUPS = T // GT
NEG_SLOTS = 4
POS_SLOTS = 2
VB = 8
VBATCHES = T // VB
FINAL_GROUP = 5
ARENA = 57376


class Arena:

    def __init__(self, memory, size):
        self.memory, self.size, self.at = memory, size, 0

    def take(self, count, dt, width):
        start, self.at = self.at, self.at + count * width
        assert self.at <= self.size, self.at
        return self.memory[:, start:self.at].bitcast(dt)


def build(nc, x, adj, w_fc, w_fc_t, b_fc, w_att, w1, w1_t, a, gamma, beta, eye, si_rows, x1_dram, out):
    with ExitStack() as ctx:
        def sb(name, shape, dt):
            return ctx.enter_context(nc.sbuf_tensor(name, shape, dt))

        def sem(name):
            return ctx.enter_context(nc.semaphore(name))

        mask = sb("mask", [P, T, T, P], U8)
        hfeat = sb("hfeat", [P, T, H, HW], F32)
        arena = sb("arena", [P, ARENA], U8)
        late = sb("late", [P, 2 * 4 * D * 4], U8)
        ident = sb("ident", [P, P], F32)
        gamma_b = sb("gamma_b", [P, D], F32)
        beta_b = sb("beta_b", [P, D], F32)
        empty = sb("empty", [P, T], F32)
        sj = sb("sj", [P, T, H], F32)
        h_sum = sb("h_sum", [P, H * HW], F32)
        stats = sb("stats", [P, 8, 6], F32)
        agg = sb("agg", [P, 6, 8], F32)
        mv = sb("mv", [P, 16], F32)
        rden = sb("rden", [P, 3, CHUNK_TILES], F32)
        ps = ctx.enter_context(nc.psum_tensor("ps", [P, 8, 512], F32))

        one = Arena(arena[:, :], ARENA)
        ring = one.take(2 * T * P, U8, 1).rearrange("p (s t i) -> p s t i", s=2, t=T)
        stage = one.take(QUARTERS * QCOLS, I32, 4).rearrange("p (q n) -> p q n", q=QUARTERS)
        G = one.take(T * G_COLS, BF16, 2).rearrange("p (t n) -> p t n", t=T)
        x_in = one.take(2 * D, F32, 4).rearrange("p (s d) -> p s d", s=2)
        hn = one.take(2 * D, F32, 4).rearrange("p (s d) -> p s d", s=2)
        hT = one.take(2 * D, F32, 4).rearrange("p (s d) -> p s d", s=2)
        num = one.take(W0, F32, 4)
        h_mean0 = one.take(D, F32, 4)
        w1_aug = one.take(D + 2 * H, F32, 4)

        two = Arena(arena[:, :], ARENA)
        V = two.take(T * 2 * 3 * HW, BF16, 2).rearrange("p (t k n) -> p t k n", t=T, k=2)
        sib = two.take(2 * CH, F32, 4).rearrange("p (s t i) -> p s t i", s=2, t=CHUNK_TILES)
        neg = two.take(NEG_SLOTS * GT * CH, U8, 1).rearrange("p (s t n) -> p s t n", s=NEG_SLOTS, t=GT)
        pos = two.take(POS_SLOTS * GT * CH, U8, 1).rearrange("p (s t n) -> p s t n", s=POS_SLOTS, t=GT)
        E = two.take(2 * 512, F32, 4).rearrange("p (s n) -> p s n", s=2)
        R = two.take(2 * CHUNK_TILES * HW, F32, 4).rearrange("p (k t n) -> p k t n", k=2, t=CHUNK_TILES)
        work = two.take(2 * VB * HW, F32, 4).rearrange("p (k t n) -> p k t n", k=2, t=VB)
        bd = two.take(T * 2 * H, F32, 4).rearrange("p (t k h) -> p t k h", t=T, k=2)
        AC = two.take(2 * T * H, F32, 4).rearrange("p (k t h) -> p k t h", k=2, t=T)
        nsj = two.take(T * H, F32, 4).rearrange("p (t h) -> p t h", t=T)
        siT = E[0:CHUNK_TILES * H, 0, :]

        tail = Arena(mask[:, 25:T, :, :].rearrange("p a b c -> p (a b c)"), 7 * T * P)
        hn_all = tail.take(8 * D, F32, 4).rearrange("p (t d) -> p t d", t=8)
        hT_all = tail.take(8 * D, F32, 4).rearrange("p (t d) -> p t d", t=8)
        Hbuf = tail.take(T * W0, F32, 4).rearrange("p (t d) -> p t d", t=T)
        wt_fc = tail.take(D, F32, 4)
        wt_1 = tail.take(D, F32, 4)
        b_bc = tail.take(D, F32, 4)
        cols = tail.take(2 * H, F32, 4)
        wdst = tail.take(1, F32, 4)
        sdst = tail.take(T, F32, 4)
        e_w = tail.take(T, F32, 4)
        x_all = hfeat[:, :, :, :].rearrange("p t h w -> p (t h w)")[:, 0:N].rearrange("p (t d) -> p t d", t=T)

        early = Arena(late[:, :], 2 * 4 * D * 4)
        mean_w = early.take(P, F32, 4)
        w_aug = early.take(W0, F32, 4)
        si = early.take(T * H, F32, 4).rearrange("p (t h) -> p t h", t=T)
        yc = late[:, :].bitcast(F32).rearrange("p (s t d) -> p s t d", s=2, t=4)

        const_in = sem("const_in")
        ones_set = sem("ones_set")
        x_piece = [sem(f"x_piece{k}") for k in range(4)]
        waug_ps, waug = sem("waug_ps"), sem("waug")
        var0, sd0, hn0, t0, hT0 = sem("var0"), sem("sd0"), sem("hn0"), sem("t0"), sem("hT0")
        hp0, hbuf, mean0 = sem("hp0"), sem("hbuf"), sem("mean0")
        mx, mx_ps, e0 = sem("mx"), sem("mx_ps"), sem("e0")
        g_f32, g_hi, g_rest, g_mid, g_ready = sem("g_f32"), sem("g_hi"), sem("g_rest"), sem("g_mid"), sem("g_ready")
        adj_in = [sem(f"adj_in{q}") for q in range(QUARTERS)]
        compared, kept = sem("compared"), sem("kept")
        rows_done, rows_read = sem("rows_done"), sem("rows_read")
        x_tile = [sem(f"x_tile{s}") for s in range(2)]
        x1_out = [sem(f"x1_out{s}") for s in range(2)]
        var1, sd1, hn1, t1, hT1 = sem("var1"), sem("sd1"), sem("hn1"), sem("t1"), sem("hT1")
        feat_ps, feat = sem("feat_ps"), sem("feat")
        si_ps, si_sb, si_out = sem("si_ps"), sem("si_sb"), sem("si_out")
        sib_in = [sem(f"sib_in{s}") for s in range(2)]
        mx1, mx1_ps, arg1, bd_ready = sem("mx1"), sem("mx1_ps"), sem("arg1"), sem("bd_ready")
        v_ready = sem("v_ready")
        signs, masks, group_done = sem("signs"), sem("masks"), sem("group_done")
        evacuated, turned, reduced, dens = sem("evacuated"), sem("turned"), sem("reduced"), sem("dens")
        h_summed, h_mean_ps, h_mean_set = sem("h_summed"), sem("h_mean_ps"), sem("h_mean_set")
        combined = sem("combined")
        x1_in = [sem(f"x1_in{s}") for s in range(2)]
        varf, sdf, final = sem("varf"), sem("sdf"), sem("final")
        out_done = [sem(f"out_done{s}") for s in range(2)]

        acc = [ps[:, 0, :], ps[:, 1, :]]
        psT = [ps[:, 2, :], ps[:, 3, :]]
        psF = [ps[:, 4, :], ps[:, 5, :]]
        psS, psM = ps[:, 6, :], ps[:, 7, :]
        CONSTS = 9 + 2 * H
        block = ctx.enter_context(nc.Block())

        def head_of(u):
            return u // CHUNKS if isinstance(u, int) else (u // CHUNKS).with_bounds(max_val=H - 1)

        def tile_of(tensor, t):
            if isinstance(t, int):
                return tensor[:, t]
            v = tensor[:, ds(t, 1)]
            return v.rearrange("p a b -> p (a b)") if len(v.shape) == 3 else v.rearrange("p a b c -> p (a b) c")

        @block.sync
        def _(sp):
            for k in range(4):
                sp.dma_start(x_all[:, 8 * k:8 * k + 8, :],
                             x[:, 8 * k * D:(8 * k + 8) * D].rearrange("p (t d) -> p t d", t=8)).then_inc(x_piece[k], 16)
            for q in range(QUARTERS):
                sp.dma_start(stage[:, q, :], adj[0, q]).then_inc(adj_in[q], 16)
            for s in range(2):
                sp.dma_start(x_in[:, s, :], x[:, s * D:(s + 1) * D]).then_inc(x_tile[s], 16)
            with sp.Fori(1, T) as t:
                for q in range(QUARTERS):
                    sp.wait_ge(compared, t * 4 + (q - 3))
                    sp.dma_start(stage[:, q, :], adj[ds(t, 1), q].rearrange("a p n -> (a p) n")).then_inc(adj_in[q], 16)

            si_by_head = si_rows.rearrange("c (t h) i -> c h t i", h=H)

            def load_si(h, c, s):
                if isinstance(h, int):
                    src = si_by_head[c, h]
                else:
                    src = si_by_head[ds(c, 1), ds(h, 1)].rearrange("a b t i -> (a b t) i")
                sp.dma_start(sib[:, s], src.partition_broadcast(P)).then_inc(sib_in[s], 16)

            sp.wait_ge(compared, 4 * T)
            sp.wait_ge(si_sb, 1)
            sp.dma_start(si_rows[0:3].rearrange("c r i -> r c i"),
                         siT[:, 0:3 * P].rearrange("r (c i) -> r c i", c=3)).then_inc(si_out, 16)
            sp.wait_ge(si_out, 16)
            load_si(0, 0, 0)
            load_si(0, 1, 1)
            sp.wait_ge(si_sb, 2)
            sp.dma_start(si_rows[3], siT[:, 3 * P:4 * P]).then_inc(si_out, 16)
            sp.wait_ge(si_out, 32)
            with sp.Fori(2, UNITS - 1, 2) as u:
                for s in range(2):
                    sp.wait_ge(masks, (u + (s - 1)) * GROUPS)
                    load_si(head_of(u + s), (u + s) % CHUNKS, s)

            def load_x1(f):
                sp.dma_start(yc[:, f % 2], x1_dram[:, 4 * f * D:4 * (f + 1) * D].rearrange("p (t d) -> p t d", t=4)).then_inc(x1_in[f % 2], 16)

            for s in range(2):
                sp.wait_ge(x1_out[s], 16 * (T // 2))
            sp.wait_ge(h_mean_set, 1)
            for f in range(2):
                load_x1(f)
            for f in range(T // 4):
                sp.wait_ge(final, f + 1)
                sp.dma_start(out[:, 4 * f * D:4 * (f + 1) * D].rearrange("p (t d) -> p t d", t=4), yc[:, f % 2]).then_inc(out_done[f % 2], 16)
                if f + 2 < T // 4:
                    sp.wait_ge(out_done[f % 2], 16 * (f // 2 + 1))
                    load_x1(f + 2)
            for s in range(2):
                sp.wait_ge(out_done[s], 16 * (T // 8))

        @block.gpsimd
        def _(pool):
            pool.memset(mean_w, 1.0 / N).then_inc(ones_set, 1)
            pool.memset(cols, 0.0).then_inc(ones_set, 1)
            pool.memset(Hbuf[:, :, D:D + 1], 1.0).then_inc(ones_set, 1)
            pool.memset(G[:, :, 3 * W0:3 * W0 + 1], 1.0).then_inc(ones_set, 1)
            pool.memset(h_sum[:, :], 0.0)
            pool.wait_ge(hn0, 4)
            pool.memset(hfeat[:, :, :, HD:HW], 1.0).then_inc(ones_set, 1)

            def keep(t, s):
                pool.wait_ge(compared, t * 4 + 4)
                if isinstance(t, int):
                    dst = mask[:, t].rearrange("p b c -> p (b c)")
                else:
                    dst = mask[:, ds(t, 1)].rearrange("p a b c -> p (a b c)")
                pool.tensor_copy(dst.bitcast(I16), ring[:, s].rearrange("p b c -> p (b c)").bitcast(I16)).then_inc(kept, 1)

            def add_to_sum(t):
                pool.drain()
                pool.wait_ge(feat, t + 1)
                if isinstance(t, int):
                    src = hfeat[:, t].rearrange("p h w -> p (h w)")
                else:
                    src = hfeat[:, ds(t, 1)].rearrange("p a h w -> p (a h w)")
                pool.tensor_tensor(h_sum[:, :], h_sum[:, :], src, ALU.add).then_inc(h_summed, 1)

            for t in range(4):
                keep(t, t % 2)
            with pool.Fori(4, T - 1, 2) as t:
                for s in range(2):
                    keep(t + s, s)
                    add_to_sum(t + (s - 4))
            for t in range(T - 4, T):
                add_to_sum(t)

            def v_batch(h, b):
                t = b * VB
                if isinstance(h, int):
                    src = hfeat[:, t:t + VB, h, :]
                    w = [bd[:, t:t + VB, k, h:h + 1] for k in range(2)]
                else:
                    src = hfeat[:, t:t + VB, ds(h, 1), :].rearrange("p t a w -> p t (a w)")
                    w = [bd[:, t:t + VB, k, ds(h, 1)] for k in range(2)]
                    pool.wait_ge(group_done, h * (CHUNKS * GROUPS) + (2 * b + 2 - GROUPS))
                part = [V[:, t:t + VB, :, k * HW:(k + 1) * HW].rearrange("p t k n -> p k t n") for k in range(3)]
                for k in range(2):
                    pool.tensor_tensor(work[:, k], src, w[k].to_broadcast([P, VB, HW]), ALU.mult)
                pool.drain()
                pool.tensor_copy(part[0], work[:, :])
                pool.drain()
                pool.tensor_tensor(work[:, :], work[:, :], part[0], ALU.subtract)
                pool.drain()
                pool.tensor_copy(part[1], work[:, :])
                pool.drain()
                pool.tensor_tensor(part[2], work[:, :], part[1], ALU.subtract).then_inc(v_ready, 1)
                pool.drain()

            def combine(h, c):
                rows = slice(c * CHUNK_TILES, (c + 1) * CHUNK_TILES)
                if isinstance(h, int):
                    ac = [AC[:, k, rows, h:h + 1] for k in range(2)]
                    mean = h_sum[:, h * HW:h * HW + HD]
                    dst = hfeat[:, rows, h, 0:HD]
                else:
                    ac = [AC[:, k, rows, ds(h, 1)] for k in range(2)]
                    mean = h_sum[:, ds(h * HW, HD)]
                    dst = hfeat[:, rows, ds(h, 1), 0:HD].rearrange("p t a w -> p t (a w)")
                shape = [P, CHUNK_TILES, HD]
                wk = work[:, 0, 0:CHUNK_TILES, 0:HD]
                pool.wait_ge(dens, h * CHUNKS + (c + 1))
                for k in range(2):
                    pool.tensor_tensor(R[:, k, :, 0:HD], R[:, k, :, 0:HD], ac[k].to_broadcast(shape), ALU.mult)
                pool.tensor_tensor(wk, mean.unsqueeze(1).to_broadcast(shape),
                                   empty[:, rows].unsqueeze(2).to_broadcast(shape), ALU.mult)
                pool.drain()
                pool.tensor_tensor(R[:, 0, :, 0:HD], R[:, 0, :, 0:HD], R[:, 1, :, 0:HD], ALU.add)
                pool.drain()
                pool.tensor_tensor(R[:, 0, :, 0:HD], R[:, 0, :, 0:HD], wk, ALU.add)
                pool.drain()
                pool.tensor_tensor(dst, R[:, 0, :, 0:HD], rden[:, 2, :].unsqueeze(2).to_broadcast(shape),
                                   ALU.mult).then_inc(combined, 1)
                pool.drain()

            pool.sem_inc(combined, 1)
            pool.wait_ge(bd_ready, 1)
            for b in range(VBATCHES):
                v_batch(0, b)
            pool.wait_ge(h_mean_set, 1)
            with pool.Fori(0, H - 1) as h:
                combine(h, 0)
                combine(h, 1)
                v_batch(h + 1, 0)
                v_batch(h + 1, 1)
                combine(h, 2)
                v_batch(h + 1, 2)
                v_batch(h + 1, 3)
                combine(h, 3)
            for c in range(CHUNKS):
                combine(H - 1, c)

        @block.scalar
        def _(act):
            act.dma_start(wt_fc, w_fc_t[:, :]).then_inc(const_in, 16)
            act.dma_start(wdst, w_att[D:2 * D, :]).then_inc(const_in, 16)
            act.dma_start(w_aug[:, 0:D], w_fc[:, :]).then_inc(const_in, 16)
            act.dma_start(ident[:, :], eye[:, :]).then_inc(const_in, 16)
            act.dma_start(b_bc, b_fc[0].partition_broadcast(P)).then_inc(const_in, 16)
            act.dma_start(w1_aug[:, 0:D], w1[:, :]).then_inc(const_in, 16)
            act.dma_start(wt_1, w1_t[:, :]).then_inc(const_in, 16)
            act.dma_start(gamma_b[:, :], gamma[0].partition_broadcast(P)).then_inc(const_in, 16)
            act.dma_start(beta_b[:, :], beta[0].partition_broadcast(P)).then_inc(const_in, 16)
            act.wait_ge(ones_set, 2)
            for h in range(H):
                for k in range(2):
                    act.dma_start(cols[h * HD:(h + 1) * HD, k * H + h:k * H + h + 1],
                                  a[k * HD:(k + 1) * HD, :]).then_inc(const_in, 16)

            for k in range(4):
                act.wait_ge(var0, k + 1)
                act.activation(agg[:, 4, :], agg[:, 3, :], ACT.Sqrt).then_inc(sd0, 1)
                for half in range(2):
                    act.wait_ge(t0, 2 * k + half + 1)
                    if k:
                        act.wait_ge(hp0, 2 * k + half - 1)
                    act.activation(hT_all[:, 4 * half:4 * half + 4].rearrange("p t d -> p (t d)"), psT[half],
                                   ACT.Relu).then_inc(hT0, 1)
            act.wait_ge(mx, 3)
            act.activation(e_w, sdst, ACT.Exp, bias=mv[:, 3:4]).then_inc(e0, 1)

            for k in range(5):
                if k < 4:
                    act.wait_ge(g_f32, k + 1)
                    act.activation(G[:, 8 * k:8 * k + 8, 0:W0], Hbuf[:, 8 * k:8 * k + 8], ACT.Copy).then_inc(g_hi, 1)
                if k:
                    act.wait_ge(g_rest, k)
                    act.activation(G[:, 8 * k - 8:8 * k, W0:2 * W0], Hbuf[:, 8 * k - 8:8 * k], ACT.Copy).then_inc(g_mid, 1)

            def tile_step(m, s, n_out):
                act.wait_ge(var1, m + 1)
                act.activation(mv[:, 6:7], mv[:, 5:6], ACT.Sqrt).then_inc(sd1, 1)
                act.dma_start(x1_dram[:, m * D:(m + 1) * D] if isinstance(m, int) else x1_dram[:, ds(m * D, D)],
                              x_in[:, s]).then_inc(x1_out[s], 16)
                if n_out is not None:
                    act.wait_ge(x1_out[1 - s], n_out)
                    act.dma_start(x_in[:, 1 - s], x[:, (m + 1) * D:(m + 2) * D] if isinstance(m, int)
                                  else x[:, ds((m + 1) * D, D)]).then_inc(x_tile[1 - s], 16)
                act.wait_ge(t1, m + 1)
                act.activation(hT[:, s], psT[s][:, 0:D], ACT.Relu).then_inc(hT1, 1)
                act.wait_ge(feat_ps, m + 1)
                if isinstance(m, int):
                    dst, d_si, d_sj = hfeat[:, m, :, 0:HD], si[:, m, :], sj[:, m, :]
                else:
                    dst = hfeat[:, ds(m, 1), :, 0:HD].rearrange("p a h w -> p (a h) w")
                    d_si, d_sj = tile_of(si, m), tile_of(sj, m)
                act.activation(d_si, psF[s][:, D:D + H], ACT.Copy)
                act.activation(d_sj, psF[s][:, D + H:D + 2 * H], ACT.Copy)
                act.activation(dst, psF[s][:, 0:D].rearrange("p (h w) -> p h w", h=H), ACT.Copy).then_inc(feat, 1)

            act.wait_ge(ones_set, 5)
            tile_step(0, 0, None)
            tile_step(1, 1, 16)
            with act.Fori(2, T - 3, 2) as m:
                tile_step(m, 0, m * 8)
                tile_step(m + 1, 1, m * 8 + 16)
            tile_step(T - 2, 0, (T - 2) * 8)
            act.wait_ge(si_ps, 1)
            act.activation(siT[:, 0:3 * P], psS[0:CHUNK_TILES * H, 0:3 * P], ACT.Copy).then_inc(si_sb, 1)
            tile_step(T - 1, 1, None)

            act.wait_ge(arg1, 1)
            act.activation(bd.rearrange("p t k h -> p (t k h)"), bd.rearrange("p t k h -> p (t k h)"), ACT.Exp).then_inc(bd_ready, 1)
            act.wait_ge(arg1, 2)
            act.activation(AC.rearrange("p k t h -> p (k t h)"), AC.rearrange("p k t h -> p (k t h)"), ACT.Exp).then_inc(bd_ready, 1)
            act.wait_ge(si_ps, 2)
            act.activation(siT[:, 3 * P:4 * P], psS[0:CHUNK_TILES * H, 3 * P:4 * P], ACT.Copy).then_inc(si_sb, 1)

            def evacuate(u, s, k):
                if k == 0:
                    act.wait_ge(group_done, (u + 1) * GROUPS)
                act.wait_ge(turned, u * 4 + (k + 1))
                act.activation(E[0:3 * HW, k % 2], ps[0:3 * HW, 4 * s + k, :], ACT.Copy).then_inc(evacuated, 1)

            def unit(u, s, hooks):
                h = head_of(u)
                act.wait_ge(sib_in[s], (u - s) * 8 + 16)
                for g in range(GROUPS):
                    for hook in hooks.get(g, ()):
                        hook()
                    if not (isinstance(u, int) and u == 0 and g < NEG_SLOTS):
                        act.wait_ge(group_done, u * GROUPS + (g - NEG_SLOTS + 1))
                    for j in range(GT - 1):
                        t = g * GT + j
                        bias = sj[:, t, h:h + 1] if isinstance(h, int) else sj[:, t, ds(h, 1)]
                        act.activation(neg[:, g % NEG_SLOTS, j].bitcast(I8), sib[:, s].rearrange("p t i -> p (t i)"),
                                       ACT.Sign, bias=bias).then_inc(signs, 1)

            def evacuations(u, s):
                return {4 + k: [lambda k=k: evacuate(u, s, k)] for k in range(4)}

            act.wait_ge(rows_done, T)
            act.wait_ge(si_out, 32)
            unit(0, 0, {})
            with act.Fori(1, UNITS - 4, 2) as u:
                unit(u, 1, evacuations(u - 1, 0))
                unit(u + 1, 0, evacuations(u, 1))
            def final_sqrt(f):
                act.wait_ge(varf, f + 1)
                act.activation(agg[:, 4, 0:4], agg[:, 3, 0:4], ACT.Sqrt).then_inc(sdf, 1)

            unit(UNITS - 3, 1, evacuations(UNITS - 4, 0))
            for c in range(2):
                u = UNITS - 2 + c
                hooks = evacuations(u - 1, 1 - c)
                hooks[FINAL_GROUP] = hooks[FINAL_GROUP] + [lambda c=c: final_sqrt(2 * c)]
                hooks[FINAL_GROUP + 1] = hooks[FINAL_GROUP + 1] + [lambda c=c: final_sqrt(2 * c + 1)]
                unit(u, c, hooks)
            final_sqrt(4)
            final_sqrt(5)
            for k in range(4):
                evacuate(UNITS - 1, 1, k)
            final_sqrt(6)
            final_sqrt(7)

        @block.tensor
        def _(pe):
            pe.wait_ge(const_in, 16 * CONSTS)
            pe.matmul(psM[:, 0:1], wt_fc, wdst, start=True, stop=True)
            pe.matmul(psM[:, 8:8 + 2 * H], wt_1, cols, start=True, stop=True).then_inc(waug_ps, 1)
            for k in range(4):
                pe.wait_ge(hn0, k + 1)
                for half in range(2):
                    if k:
                        pe.wait_ge(hT0, 2 * k + half - 1)
                    for i in range(4):
                        ins = pe.transpose(psT[half][:, i * P:(i + 1) * P], hn_all[:, 4 * half + i], ident[:, :])
                    ins.then_inc(t0, 1)
                if k == 0:
                    pe.wait_ge(waug, 1)
                for half in range(2):
                    pe.wait_ge(hT0, 2 * k + half + 1)
                    if k:
                        pe.wait_ge(hbuf, 2 * k + half - 1)
                    for i in range(4):
                        pe.matmul(psF[half][:, i * D:(i + 1) * D], hT_all[:, 4 * half + i], w_aug[:, 0:D], start=True, stop=True)
                    for i in range(4):
                        t = 8 * k + 4 * half + i
                        ins = pe.matmul(psS[:, t:t + 1], hT_all[:, 4 * half + i], w_aug[:, D:W0], start=True, stop=True)
                    ins.then_inc(hp0, 1)

            def mean_of(m):
                pe.wait_ge(hbuf, m + 1)
                pe.matmul(psT[0], mean_w, Hbuf[:, 4 * m:4 * m + 4, 0:D], start=(m == 0), stop=(m == 7)).then_inc(mean0, 1)

            for m in range(4):
                mean_of(m)
            pe.wait_ge(mx, 1)
            pe.transpose(psM[0:1, 0:P], mv[:, 0:1], ident[:, :]).then_inc(mx_ps, 1)
            pe.wait_ge(mx, 2)
            pe.matmul(psM[:, P:P + 1], mean_w[0:1, :], mv[0:1, 2:3], start=True, stop=True).then_inc(mx_ps, 1)
            for m in range(4, 8):
                mean_of(m)

            def rows(t, s, post):
                pe.wait_ge(compared, t * 4 + 4)
                if not (isinstance(t, int) and t < 2):
                    pe.wait_ge(rows_read, t - 1)
                pe.nop(nofuse=True)
                for j in range(T):
                    if isinstance(t, int) and t == 0 and j % 8 == 0:
                        pe.wait_ge(g_ready, j // 8 + 1)
                        pe.nop(nofuse=True)
                    ins = pe.matmul(acc[s][:, 0:G_COLS], ring[:, s, j].bitcast(FP8), G[:, j, :],
                                    start=(j == 0), stop=(j == T - 1))
                    if j == 10 and post is not None:
                        turn(post, s)
                    if j == 24 and post is not None:
                        features(post, s)
                        pe.nop(nofuse=True)
                ins.then_inc(rows_done, 1)

            def turn(m, s):
                pe.wait_ge(hn1, m + 1)
                pe.transpose(psT[s][:, 0:D], hn[:, s], ident[:, :]).then_inc(t1, 1)

            def features(m, s):
                pe.wait_ge(hT1, m + 1)
                pe.matmul(psF[s][:, 0:D + 2 * H], hT[:, s], w1_aug, start=True, stop=True).then_inc(feat_ps, 1)

            def turn_si(c):
                return pe.transpose(psS[0:CHUNK_TILES * H, c * P:(c + 1) * P],
                                    si[:, c * CHUNK_TILES:(c + 1) * CHUNK_TILES, :].rearrange("p t h -> p (t h)"), ident[:, :])

            rows(0, 0, None)
            rows(1, 1, None)
            with pe.Fori(2, T - 1, 2) as t:
                for s in range(2):
                    rows(t + s, s, t + (s - 2))
            pe.wait_ge(feat, 3 * CHUNK_TILES)
            for c in range(3):
                ins = turn_si(c)
            ins.then_inc(si_ps, 1)
            for s in range(2):
                turn(T - 2 + s, s)
                features(T - 2 + s, s)
            pe.wait_ge(mx1, 1)
            pe.transpose(psM[0:H, 0:P], mv[:, 0:H], ident[:, :]).then_inc(mx1_ps, 1)
            pe.wait_ge(mx1, 2)
            pe.matmul(psM[:, P:P + H], mean_w[0:H, :], mv[0:H, 8:8 + H], start=True, stop=True).then_inc(mx1_ps, 1)
            turn_si(3).then_inc(si_ps, 1)

            def turn_bank(u, s, k):
                pe.wait_ge(evacuated, u * 4 + (k + 1))
                for i in range(4):
                    ins = pe.transpose(ps[:, 4 * s + k, i * 3 * HW:(i + 1) * 3 * HW],
                                       E[0:3 * HW, k % 2, i * P:(i + 1) * P], ident[0:3 * HW, 0:3 * HW])
                ins.then_inc(turned, 1)

            def unit(u, s, hooks):
                h = head_of(u)
                if not (isinstance(u, int) and u == 0):
                    pe.wait_ge(reduced, u * 4 - 3)
                for g in range(GROUPS):
                    pe.wait_ge(masks, u * GROUPS + (g + 1))
                    if g % 2 == 0:
                        pe.wait_ge(v_ready, h * VBATCHES + (g // 2 + 1))
                    pe.nop(nofuse=True)
                    for j in range(GT):
                        t = g * GT + j
                        for k, m in enumerate((pos[:, g % POS_SLOTS, j], neg[:, g % NEG_SLOTS, j])):
                            for half in range(2):
                                ins = pe.matmul(ps[0:3 * HW, 4 * s + 2 * k + half, :], V[:, t, k, :],
                                                m[:, half * 512:(half + 1) * 512].bitcast(FP8),
                                                start=(t == 0), stop=(t == T - 1))
                    ins.then_inc(group_done, 1)
                    for hook in hooks.get(g, ()):
                        hook()

            def turns(u, s):
                return {1 + k: [lambda k=k: turn_bank(u, s, k)] for k in range(4)}

            def mean_of_h():
                pe.wait_ge(h_summed, T)
                pe.matmul(ps[:, 4, 0:H * HW], mean_w, h_sum[:, :], start=True, stop=True).then_inc(h_mean_ps, 1)

            pe.wait_ge(arg1, 1)
            pe.wait_ge(si_sb, 2)
            pe.sem_inc(turned, 2)
            unit(0, 0, {GROUPS - 2: [mean_of_h]})
            pe.wait_ge(h_mean_set, 1)
            with pe.Fori(1, UNITS - 2, 2) as u:
                unit(u, 1, turns(u - 1, 0))
                unit(u + 1, 0, turns(u, 1))
            unit(UNITS - 1, 1, turns(UNITS - 2, 0))
            for k in range(4):
                turn_bank(UNITS - 1, 1, k)

        @block.vector
        def _(dve):
            def compare(t, s):
                for q in range(QUARTERS):
                    dve.wait_ge(adj_in[q], t * 16 + 16)
                    if q == 0 and not (isinstance(t, int) and t < 2):
                        dve.wait_ge(rows_done, t - 1)
                        dve.wait_ge(kept, t - 1)
                    dve.tensor_scalar(ring[:, s, 8 * q:8 * q + 8].rearrange("p a b -> p (a b)").bitcast(I8), stage[:, q, :],
                                      0.0, float(ONE_FP8), ALU.is_gt, ALU.mult).then_inc(compared, 1)

            def row_stats(n):
                m_even, m_odd = stats[:, 0:n, 1], stats[:, 0:n, 4]
                dve.drain()
                dve.tensor_tensor(agg[:, 0, 0:n], m_even, m_odd, ALU.add)
                dve.tensor_tensor(agg[:, 1, 0:n], m_even, m_odd, ALU.subtract)
                dve.tensor_tensor(agg[:, 2, 0:n], stats[:, 0:n, 2], stats[:, 0:n, 5], ALU.add)
                dve.drain()
                dve.tensor_tensor(agg[:, 1, 0:n], agg[:, 1, 0:n], agg[:, 1, 0:n], ALU.mult)
                dve.tensor_scalar(agg[:, 0, 0:n], agg[:, 0, 0:n], 0.5, None, ALU.mult)
                dve.drain()
                dve.scalar_tensor_tensor(agg[:, 2, 0:n], agg[:, 1, 0:n], D / 4.0, agg[:, 2, 0:n], ALU.mult, ALU.add)
                dve.drain()
                return dve.tensor_scalar(agg[:, 3, 0:n], agg[:, 2, 0:n], 1.0 / D, EPS, ALU.mult, ALU.add)

            def h_out(k, half):
                dve.wait_ge(hp0, 2 * k + half + 1)
                t = 8 * k + 4 * half
                dve.tensor_tensor(Hbuf[:, t:t + 4, 0:D], psF[half].rearrange("p (t d) -> p t d", t=4),
                                  b_bc.unsqueeze(1).to_broadcast([P, 4, D]), ALU.add).then_inc(hbuf, 1)

            for k in range(4):
                dve.wait_ge(x_piece[k], 16)
                if k:
                    dve.wait_ge(sd0, k)
                for i in range(8):
                    dve.bn_stats(stats[:, i, :], x_all[:, 8 * k + i, :])
                row_stats(8).then_inc(var0, 1)
                if k == 0:
                    dve.wait_ge(waug_ps, 1)
                    dve.tensor_copy(w_aug[:, D:W0], psM[:, 0:1])
                    dve.tensor_copy(w1_aug[:, D:D + 2 * H], psM[:, 8:8 + 2 * H]).then_inc(waug, 1)
                else:
                    for half in range(2):
                        h_out(k - 1, half)
                dve.wait_ge(sd0, k + 1)
                dve.reciprocal(agg[:, 5, :], agg[:, 4, :])
                dve.drain()
                if k:
                    dve.wait_ge(t0, 2 * k)
                for i in range(8):
                    ins = dve.tensor_scalar(hn_all[:, i], x_all[:, 8 * k + i, :], agg[:, 0, i:i + 1], agg[:, 5, i:i + 1],
                                            ALU.subtract, ALU.mult)
                ins.then_inc(hn0, 1)
            for half in range(2):
                h_out(3, half)
            dve.tensor_copy(sdst, psS[:, 0:T])
            dve.drain()
            dve.reduce_max(mv[:, 0:1], sdst, X_AXIS).then_inc(mx, 1)
            dve.wait_ge(mx_ps, 1)
            dve.reduce_max(mv[0:1, 1:2], psM[0:1, 0:P], X_AXIS)
            dve.drain()
            dve.tensor_scalar(mv[0:1, 2:3], mv[0:1, 1:2], float(N), None, ALU.mult).then_inc(mx, 1)
            dve.wait_ge(mx_ps, 2)
            dve.tensor_scalar(mv[:, 3:4], psM[:, P:P + 1], -1.0, EXP_SHIFT, ALU.mult, ALU.add).then_inc(mx, 1)
            compare(0, 0)
            dve.wait_ge(ones_set, 4)
            for step in range(6):
                if step < 4:
                    g = Hbuf[:, 8 * step:8 * step + 8]
                    dve.wait_ge(e0, 1)
                    dve.wait_ge(mean0, 2 * step + 2)
                    dve.tensor_tensor(g, g, e_w[:, 8 * step:8 * step + 8].unsqueeze(2).to_broadcast([P, 8, W0]),
                                      ALU.mult).then_inc(g_f32, 1)
                if 1 <= step < 5:
                    g = Hbuf[:, 8 * step - 8:8 * step]
                    dve.wait_ge(g_hi, step)
                    dve.tensor_tensor(g, g, G[:, 8 * step - 8:8 * step, 0:W0], ALU.subtract).then_inc(g_rest, 1)
                if step >= 2:
                    dve.wait_ge(g_mid, step - 1)
                    dve.tensor_tensor(G[:, 8 * step - 16:8 * step - 8, 2 * W0:3 * W0], Hbuf[:, 8 * step - 16:8 * step - 8],
                                      G[:, 8 * step - 16:8 * step - 8, W0:2 * W0], ALU.subtract).then_inc(g_ready, 1)
            dve.wait_ge(mean0, 8)
            dve.tensor_reduce(h_mean0, psT[0].rearrange("p (t d) -> p d t", t=4), X_AXIS, ALU.add)

            def rows_out(m, s, n_in):
                e_m = empty[:, m:m + 1] if isinstance(m, int) else empty[:, ds(m, 1)]
                dve.wait_ge(rows_done, m + 1)
                dve.tensor_reduce(num, acc[s][:, 0:3 * W0].rearrange("p (k c) -> p c k", k=3), X_AXIS, ALU.add)
                dve.tensor_scalar(e_m, acc[s][:, 3 * W0:3 * W0 + 1], 0.5, None, ALU.is_lt).then_inc(rows_read, 1)
                dve.drain()
                dve.tensor_tensor(mv[:, 0:1], num[:, D:W0], e_m, ALU.add)
                dve.scalar_tensor_tensor(num[:, 0:D], h_mean0, e_m, num[:, 0:D], ALU.mult, ALU.add)
                dve.drain()
                dve.reciprocal(mv[:, 1:2], mv[:, 0:1])
                dve.drain()
                dve.wait_ge(x_tile[s], n_in)
                dve.scalar_tensor_tensor(x_in[:, s], num[:, 0:D], mv[:, 1:2], x_in[:, s], ALU.mult, ALU.add)
                dve.drain()
                dve.bn_stats(stats[:, 0, :], x_in[:, s])
                dve.drain()
                dve.bn_aggr(mv[:, 2:4], stats[:, 0, :])
                dve.drain()
                dve.tensor_scalar(mv[:, 5:6], mv[:, 3:4], EPS, None, ALU.add).then_inc(var1, 1)
                dve.wait_ge(sd1, m + 1)
                dve.reciprocal(mv[:, 4:5], mv[:, 6:7])
                dve.drain()
                dve.tensor_scalar(hn[:, s], x_in[:, s], mv[:, 2:3], mv[:, 4:5], ALU.subtract, ALU.mult).then_inc(hn1, 1)

            compare(1, 1)
            with dve.Fori(2, T - 1, 2) as t:
                for s in range(2):
                    compare(t + s, s)
                    rows_out(t + (s - 2), s, t * 8)
            for s in range(2):
                rows_out(T - 2 + s, s, 16 * (T // 2))

            dve.wait_ge(feat, T)
            dve.drain()
            dve.tensor_reduce(mv[:, 0:H], sj[:, :, :].rearrange("p t h -> p h t"), X_AXIS, ALU.max).then_inc(mx1, 1)
            dve.wait_ge(mx1_ps, 1)
            dve.reduce_max(mv[0:H, 4:5], psM[0:H, 0:P], X_AXIS)
            dve.drain()
            dve.tensor_scalar(mv[0:H, 8:8 + H], ident[0:H, 0:H], mv[0:H, 4:5], float(N), ALU.mult, ALU.mult).then_inc(mx1, 1)
            dve.wait_ge(mx1_ps, 2)
            sj_max = psM[:, P:P + H].unsqueeze(1).to_broadcast([P, T, H])
            dve.tensor_tensor(bd[:, :, 0, :], sj[:, :, :], sj_max, ALU.subtract)
            dve.tensor_tensor(AC[:, 0], si[:, :, :], sj_max, ALU.add)
            dve.drain()
            dve.tensor_scalar(bd[:, :, 1, :], bd[:, :, 0, :], ALPHA, EXP_SHIFT, ALU.mult, ALU.add)
            dve.drain()
            dve.tensor_scalar(bd[:, :, 0, :], bd[:, :, 0, :], EXP_SHIFT, None, ALU.add).then_inc(arg1, 1)
            dve.tensor_scalar(AC[:, 1], AC[:, 0], ALPHA - 1.0, 0.0, ALU.mult, ALU.min)
            dve.drain()
            dve.tensor_scalar(AC[:, 0], AC[:, 0], 1.0 - ALPHA, 0.0, ALU.mult, ALU.min).then_inc(arg1, 1)
            dve.tensor_scalar(nsj, sj[:, :, :], -1.0, None, ALU.mult)
            dve.drain()

            def reduce_bank(u, s, k):
                dve.wait_ge(turned, u * 4 + (k + 3))
                if k == 0:
                    dve.wait_ge(combined, u + 1)
                dve.tensor_reduce(R[:, k // 2, 4 * (k % 2):4 * (k % 2) + 4],
                                  ps[:, 4 * s + k, 0:4 * 3 * HW].rearrange("p (t k c) -> p t c k", t=4, k=3),
                                  X_AXIS, ALU.add).then_inc(reduced, 1)

            def denominators(u):
                c, h = u % CHUNKS, head_of(u)
                for k in range(2):
                    if isinstance(u, int):
                        ac = AC[:, k, c * CHUNK_TILES:(c + 1) * CHUNK_TILES, h]
                    else:
                        ac = AC[:, k, ds(c * CHUNK_TILES, CHUNK_TILES), ds(h, 1)].rearrange("p t a -> p (t a)")
                    if k == 0:
                        dve.drain()
                    dve.tensor_tensor(rden[:, k, :], R[:, k, :, HD], ac, ALU.mult)
                e_rows = (empty[:, c * CHUNK_TILES:(c + 1) * CHUNK_TILES] if isinstance(u, int)
                          else empty[:, ds(c * CHUNK_TILES, CHUNK_TILES)])
                dve.drain()
                dve.tensor_tensor(rden[:, 0, :], rden[:, 0, :], rden[:, 1, :], ALU.add)
                dve.drain()
                dve.tensor_tensor(rden[:, 0, :], rden[:, 0, :], e_rows, ALU.add)
                dve.drain()
                dve.reciprocal(rden[:, 2, :], rden[:, 0, :]).then_inc(dens, 1)

            def unit(u, s, hooks):
                c, h = u % CHUNKS, head_of(u)
                dve.wait_ge(sib_in[s], (u - s) * 8 + 16)
                for g in range(GROUPS):
                    for hook in hooks.get(g, ()):
                        hook()
                    n_slot, p_slot = neg[:, g % NEG_SLOTS], pos[:, g % POS_SLOTS]
                    first = isinstance(u, int) and u == 0
                    if not (first and g < NEG_SLOTS):
                        dve.wait_ge(group_done, u * GROUPS + (g - NEG_SLOTS + 1))
                    t = g * GT + GT - 1
                    bias = nsj[:, t, h:h + 1] if isinstance(h, int) else nsj[:, t, ds(h, 1)]
                    dve.tensor_scalar(n_slot[:, GT - 1].bitcast(I8), sib[:, s].rearrange("p t i -> p (t i)"), bias, -1.0,
                                      ALU.is_lt, ALU.mult)
                    dve.drain()
                    dve.wait_ge(signs, (u * GROUPS + (g + 1)) * (GT - 1))
                    if isinstance(u, int):
                        m = mask[:, c * CHUNK_TILES:(c + 1) * CHUNK_TILES, g * GT:(g + 1) * GT, :]
                    else:
                        m = mask[:, ds(c * CHUNK_TILES, CHUNK_TILES), g * GT:(g + 1) * GT, :]
                    m = m.bitcast(U32).rearrange("p i j n -> p j i n")
                    nv = n_slot.bitcast(U32).rearrange("p j (i n) -> p j i n", i=CHUNK_TILES)
                    pv = p_slot.bitcast(U32).rearrange("p j (i n) -> p j i n", i=CHUNK_TILES)
                    dve.tensor_tensor(nv, nv, m, ALU.bitwise_and)
                    dve.drain()
                    if not (first and g < POS_SLOTS):
                        dve.wait_ge(group_done, u * GROUPS + (g - POS_SLOTS + 1))
                    dve.tensor_tensor(pv, nv, m, ALU.bitwise_xor).then_inc(masks, 1)

            def reductions(u, s):
                return {4 + k: [lambda k=k: reduce_bank(u, s, k)] for k in range(4)}

            def final_rows(f):
                o = hfeat[:, 4 * f:4 * f + 4, :, 0:HD]
                dve.wait_ge(combined, UNITS - CHUNKS + f // 2 + 2)
                if f:
                    dve.wait_ge(sdf, f)
                dve.drain()
                for i in range(4):
                    dve.bn_stats(stats[:, i, :], o[:, i])
                row_stats(4).then_inc(varf, 1)
                dve.wait_ge(sdf, f + 1)
                dve.reciprocal(agg[:, 5, 0:4], agg[:, 4, 0:4])
                dve.drain()
                for i in range(4):
                    dve.tensor_scalar(o[:, i], o[:, i], agg[:, 0, i:i + 1], agg[:, 5, i:i + 1], ALU.subtract, ALU.mult)
                dve.drain()
                gb = gamma_b[:, :].rearrange("p (h w) -> p h w", h=H).unsqueeze(1).to_broadcast([P, 4, H, HD])
                dve.tensor_tensor(o, o, gb, ALU.mult)
                dve.wait_ge(x1_in[f % 2], 16 * (f // 2 + 1))
                y = yc[:, f % 2]
                dve.tensor_tensor(y, y, beta_b[:, :].unsqueeze(1).to_broadcast([P, 4, D]), ALU.add)
                dve.drain()
                y4 = y.rearrange("p t (h w) -> p t h w", h=H)
                dve.tensor_tensor(y4, y4, o, ALU.add).then_inc(final, 1)

            def set_h_mean():
                dve.wait_ge(h_mean_ps, 1)
                dve.tensor_copy(h_sum[:, :], ps[:, 4, 0:H * HW]).then_inc(h_mean_set, 1)

            dve.sem_inc(reduced, 1)
            for s in range(2):
                dve.wait_ge(x1_out[s], 16 * (T // 2))
            dve.wait_ge(rows_done, T)
            unit(0, 0, {})
            set_h_mean()
            with dve.Fori(1, UNITS - 4, 2) as u:
                unit(u, 1, reductions(u - 1, 0))
                denominators(u - 1)
                unit(u + 1, 0, reductions(u, 1))
                denominators(u)
            unit(UNITS - 3, 1, reductions(UNITS - 4, 0))
            denominators(UNITS - 4)
            for c in range(2):
                u = UNITS - 2 + c
                hooks = reductions(u - 1, 1 - c)
                hooks[FINAL_GROUP] = hooks[FINAL_GROUP] + [lambda c=c: final_rows(2 * c)]
                hooks[FINAL_GROUP + 1] = hooks[FINAL_GROUP + 1] + [lambda c=c: final_rows(2 * c + 1)]
                unit(u, c, hooks)
                denominators(u - 1)
            final_rows(4)
            final_rows(5)
            for k in range(4):
                reduce_bank(UNITS - 1, 1, k)
            denominators(UNITS - 1)
            final_rows(6)
            final_rows(7)


def kernel(x, adj, L0_gnn_W_fc, L0_gnn_b_fc, L0_gnn_w_att, L0_gnn_b_att, L1_gnn_W, L1_gnn_a, L1_gnn_gamma, L1_gnn_beta):
    import concourse.bacc as bacc
    from concourse.bass_utils import run_bass_kernel_spmd

    c = np.ascontiguousarray
    adj = np.asarray(adj).reshape(P, T, P, T).transpose(1, 3, 2, 0)
    adj = adj.reshape(T, QUARTERS, T // QUARTERS, P, P).transpose(0, 1, 3, 2, 4)
    ins = {
        "x": c(x).reshape(P, N),
        "adj": c(adj).reshape(T, QUARTERS, P, QCOLS),
        "w_fc": c(L0_gnn_W_fc),
        "w_fc_t": c(np.asarray(L0_gnn_W_fc).T),
        "b_fc": c(L0_gnn_b_fc).reshape(1, D),
        "w_att": c(L0_gnn_w_att).reshape(2 * D, 1),
        "w1": c(L1_gnn_W),
        "w1_t": c(np.asarray(L1_gnn_W).T),
        "a": c(L1_gnn_a),
        "gamma": c(L1_gnn_gamma).reshape(1, D),
        "beta": c(L1_gnn_beta).reshape(1, D),
        "eye": np.eye(P, dtype=np.float32),
    }
    nc = bacc.Bacc("TRN2", target_bir_lowering=False, num_devices=1)
    aps = [nc.dram_tensor(f"in_{k}", v.shape, mybir.dt.from_np(v.dtype), kind="ExternalInput").ap() for k, v in ins.items()]
    si_rows = nc.dram_tensor("si_rows", (CHUNKS, CHUNK_TILES * H, P), F32, kind="Internal").ap()
    x1_dram = nc.dram_tensor("x1_rows", (P, N), F32, kind="Internal").ap()
    out = nc.dram_tensor("out_rows", (P, N), F32, kind="ExternalOutput").ap()
    build(nc, *aps, si_rows, x1_dram, out)
    r = run_bass_kernel_spmd(nc, [{f"in_{k}": v for k, v in ins.items()}], core_ids=[0])
    return r.results[0]["out_rows"].reshape(N, D)
```

```python
import numpy as np
from contextlib import ExitStack
import concourse.bass as bass
from concourse import mybir

ALU = mybir.AluOpType
ACT = mybir.ActivationFunctionType
X_AXIS = mybir.AxisListType.X
F32, BF16, FP8 = mybir.dt.float32, mybir.dt.bfloat16, mybir.dt.float8e4
I32, U32, I16, I8, U8 = mybir.dt.int32, mybir.dt.uint32, mybir.dt.int16, mybir.dt.int8, mybir.dt.uint8
ds = bass.ds

P = 128
N = 4096
T = N // P
D = 128
H = 4
HD = D // H
HW = HD + 1
ALPHA = 0.2
EPS = 1e-5
EXP_SHIFT = 60.0
ONE_FP8 = 0x38

W0 = D + 1
G_COLS = 3 * W0 + 1
QUARTERS = 4
QCOLS = T // QUARTERS * P

CHUNK_TILES = 8
CHUNKS = T // CHUNK_TILES
CH = CHUNK_TILES * P
UNITS = H * CHUNKS
GT = 4
GROUPS = T // GT
NEG_SLOTS = 4
POS_SLOTS = 2
VB = 8
VBATCHES = T // VB
LEAD = 4
PIECE = 8
PIECES = T // PIECE
FINAL_GROUP = 6
COMBINE_STEPS = 5
ARENA = 57376


class Arena:

    def __init__(self, memory, size):
        self.memory, self.size, self.at = memory, size, 0

    def take(self, count, dt, width):
        start, self.at = self.at, self.at + count * width
        assert self.at <= self.size, self.at
        return self.memory[:, start:self.at].bitcast(dt)


def build(nc, x, adj, w_fc, w_fc_t, b_fc, w_att, w1, w1_t, a, gamma, beta, eye, si_rows, x1_dram, out):
    with ExitStack() as ctx:
        def sb(name, shape, dt):
            return ctx.enter_context(nc.sbuf_tensor(name, shape, dt))

        def sem(name):
            return ctx.enter_context(nc.semaphore(name))

        mask = sb("mask", [P, T, T, P], U8)
        hfeat = sb("hfeat", [P, T, H, HW], F32)
        arena = sb("arena", [P, ARENA], U8)
        late = sb("late", [P, 2 * 4 * D * 4], U8)
        ident = sb("ident", [P, P], F32)
        gamma_b = sb("gamma_b", [P, D], F32)
        beta_b = sb("beta_b", [P, D], F32)
        empty = sb("empty", [P, T], F32)
        sj = sb("sj", [P, T, H], F32)
        h_sum = sb("h_sum", [P, H * HW], F32)
        stats = sb("stats", [P, 8, 6], F32)
        agg = sb("agg", [P, 6, 8], F32)
        mv = sb("mv", [P, 16], F32)
        rden = sb("rden", [P, 3, CHUNK_TILES], F32)
        ps = ctx.enter_context(nc.psum_tensor("ps", [P, 8, 512], F32))

        one = Arena(arena[:, :], ARENA)
        ring = one.take(2 * T * P, U8, 1).rearrange("p (s t i) -> p s t i", s=2, t=T)
        stage = one.take(QUARTERS * QCOLS, I32, 4).rearrange("p (q n) -> p q n", q=QUARTERS)
        G = one.take(T * G_COLS, BF16, 2).rearrange("p (t n) -> p t n", t=T)
        x1_beta = one.take(2 * D, F32, 4).rearrange("p (s d) -> p s d", s=2)
        x_in = one.take(2 * D, F32, 4).rearrange("p (s d) -> p s d", s=2)
        hn = one.take(2 * D, F32, 4).rearrange("p (s d) -> p s d", s=2)
        hT = one.take(2 * D, F32, 4).rearrange("p (s d) -> p s d", s=2)
        num = one.take(W0, F32, 4)
        h_mean0 = one.take(D, F32, 4)
        w1_aug = one.take(D + 2 * H, F32, 4)

        two = Arena(arena[:, :], ARENA)
        V = two.take(T * 2 * 3 * HW, BF16, 2).rearrange("p (t k n) -> p t k n", t=T, k=2)
        sib = two.take(2 * CH, F32, 4).rearrange("p (s t i) -> p s t i", s=2, t=CHUNK_TILES)
        neg = two.take(NEG_SLOTS * GT * CH, U8, 1).rearrange("p (s t n) -> p s t n", s=NEG_SLOTS, t=GT)
        pos = two.take(POS_SLOTS * GT * CH, U8, 1).rearrange("p (s t n) -> p s t n", s=POS_SLOTS, t=GT)
        E = two.take(2 * 512, F32, 4).rearrange("p (s n) -> p s n", s=2)
        R = two.take(2 * CHUNK_TILES * HW, F32, 4).rearrange("p (k t n) -> p k t n", k=2, t=CHUNK_TILES)
        work = two.take(2 * VB * HW, F32, 4).rearrange("p (k t n) -> p k t n", k=2, t=VB)
        bd = two.take(T * 2 * H, F32, 4).rearrange("p (t k h) -> p t k h", t=T, k=2)
        AC = two.take(2 * T * H, F32, 4).rearrange("p (k t h) -> p k t h", k=2, t=T)
        nsj = two.take(T * H, F32, 4).rearrange("p (t h) -> p t h", t=T)
        siT = E[0:CHUNK_TILES * H, 0, :]

        tail = Arena(mask[:, 25:T, :, :].rearrange("p a b c -> p (a b c)"), 7 * T * P)
        hn_all = tail.take(8 * D, F32, 4).rearrange("p (t d) -> p t d", t=8)
        hT_all = tail.take(8 * D, F32, 4).rearrange("p (t d) -> p t d", t=8)
        Hbuf = tail.take(T * W0, F32, 4).rearrange("p (t d) -> p t d", t=T)
        wt_fc = tail.take(D, F32, 4)
        wt_1 = tail.take(D, F32, 4)
        b_aug = tail.take(W0, F32, 4)
        cols = tail.take(2 * H, F32, 4)
        wdst = tail.take(1, F32, 4)
        e_w = tail.take(T, F32, 4)
        stats0 = tail.take(PIECE * 6, F32, 4).rearrange("p (t n) -> p t n", t=PIECE)
        agg0 = [tail.take(6 * PIECE, F32, 4).rearrange("p (n t) -> p n t", n=6) for _ in range(PIECES)]
        x_all = hfeat[:, :, :, :].rearrange("p t h w -> p (t h w)")[:, 0:N].rearrange("p (t d) -> p t d", t=T)

        early = Arena(late[:, :], 2 * 4 * D * 4)
        mean_w = early.take(P, F32, 4)
        w_aug = early.take(W0, F32, 4)
        si = early.take(T * H, F32, 4).rearrange("p (t h) -> p t h", t=T)
        yc = late[:, :].bitcast(F32).rearrange("p (s t d) -> p s t d", s=2, t=4)

        const_in, const_late = sem("const_in"), sem("const_late")
        ones_set = sem("ones_set")
        x_piece = [sem(f"x_piece{k}") for k in range(4)]
        waug_ps, waug, w1aug_ps, w1aug = sem("waug_ps"), sem("waug"), sem("w1aug_ps"), sem("w1aug")
        var0, sd0, hn0, t0, hT0 = sem("var0"), sem("sd0"), sem("hn0"), sem("t0"), sem("hT0")
        hp0, hbuf, mean0 = sem("hp0"), sem("hbuf"), sem("mean0")
        mx, mx_ps, e0 = sem("mx"), sem("mx_ps"), sem("e0")
        g_f32, g_hi, g_rest, g_mid, g_ready = sem("g_f32"), sem("g_hi"), sem("g_rest"), sem("g_mid"), sem("g_ready")
        adj_in = [sem(f"adj_in{q}") for q in range(QUARTERS)]
        compared, in_ring = sem("compared"), sem("in_ring")
        rows_done, rows_read = sem("rows_done"), sem("rows_read")
        x_tile = [sem(f"x_tile{s}") for s in range(2)]
        x1_out = [sem(f"x1_out{s}") for s in range(2)]
        x1_plus, num_set = sem("x1_plus"), sem("num_set")
        var1, sd1, hn1, t1, hT1 = sem("var1"), sem("sd1"), sem("hn1"), sem("t1"), sem("hT1")
        feat_ps, feat = sem("feat_ps"), sem("feat")
        si_ps, si_sb, si_out = sem("si_ps"), sem("si_sb"), sem("si_out")
        sib_in = [sem(f"sib_in{s}") for s in range(2)]
        mx1, mx1_ps, arg1, bd_ready = sem("mx1"), sem("mx1_ps"), sem("arg1"), sem("bd_ready")
        v_f32, v_hi, v_rest, v_mid, v_ready = sem("v_f32"), sem("v_hi"), sem("v_rest"), sem("v_mid"), sem("v_ready")
        signs, own_signs, negs, masks, group_done = sem("signs"), sem("own_signs"), sem("negs"), sem("masks"), sem("group_done")
        evacuated, turned, reduced = sem("evacuated"), sem("turned"), sem("reduced")
        h_summed, h_mean_ps, h_mean_set = sem("h_summed"), sem("h_mean_ps"), sem("h_mean_set")
        combine_step = sem("combine_step")
        x1_in = [sem(f"x1_in{s}") for s in range(2)]
        varf, sdf, final = sem("varf"), sem("sdf"), sem("final")
        out_done = [sem(f"out_done{s}") for s in range(2)]

        acc = [ps[:, 0, :], ps[:, 1, :]]
        psT = [ps[:, 2, :], ps[:, 3, :]]
        psF = [ps[:, 4, :], ps[:, 5, :]]
        psS, psM = ps[:, 6, :], ps[:, 7, :]
        h_banks = [0, 4]
        CONSTS, LATE_CONSTS = 5, 4 + 2 * H
        block = ctx.enter_context(nc.Block())

        def head_of(u):
            return u // CHUNKS if isinstance(u, int) else (u // CHUNKS).with_bounds(max_val=H - 1)

        def tile_of(tensor, t):
            if isinstance(t, int):
                return tensor[:, t]
            v = tensor[:, ds(t, 1)]
            return v.rearrange("p a b -> p (a b)") if len(v.shape) == 3 else v.rearrange("p a b c -> p (a b) c")

        def v_part(b, k):
            return V[:, b * VB:(b + 1) * VB, :, k * HW:(k + 1) * HW].rearrange("p t k n -> p k t n")

        @block.sync
        def _(sp):
            for k in range(4):
                sp.dma_start(x_all[:, 8 * k:8 * k + 8, :],
                             x[:, 8 * k * D:(8 * k + 8) * D].rearrange("p (t d) -> p t d", t=8)).then_inc(x_piece[k], 16)
            for q in range(QUARTERS):
                sp.dma_start(stage[:, q, :], adj[0, q]).then_inc(adj_in[q], 16)
            for dst, src in ((w1_aug[:, 0:D], w1[:, :]), (wt_1, w1_t[:, :]), (gamma_b[:, :], gamma[0].partition_broadcast(P)),
                             (beta_b[:, :], beta[0].partition_broadcast(P))):
                sp.dma_start(dst, src).then_inc(const_late, 16)
            sp.wait_ge(ones_set, 2)
            for h in range(H):
                for k in range(2):
                    sp.dma_start(cols[h * HD:(h + 1) * HD, k * H + h:k * H + h + 1],
                                 a[k * HD:(k + 1) * HD, :]).then_inc(const_late, 16)
            for s in range(2):
                sp.dma_start(x_in[:, s, :], x[:, s * D:(s + 1) * D]).then_inc(x_tile[s], 16)
            with sp.Fori(1, T) as t:
                for q in range(QUARTERS):
                    sp.wait_ge(compared, t * 4 + (q - 3))
                    sp.dma_start(stage[:, q, :], adj[ds(t, 1), q].rearrange("a p n -> (a p) n")).then_inc(adj_in[q], 16)

            si_by_head = si_rows.rearrange("c (t h) i -> c h t i", h=H)

            def load_si(h, c, s):
                if isinstance(h, int):
                    src = si_by_head[c, h]
                else:
                    src = si_by_head[ds(c, 1), ds(h, 1)].rearrange("a b t i -> (a b t) i")
                sp.dma_start(sib[:, s], src.partition_broadcast(P)).then_inc(sib_in[s], 16)

            sp.wait_ge(compared, 4 * T)
            sp.wait_ge(si_sb, 1)
            sp.dma_start(si_rows[0:3].rearrange("c r i -> r c i"),
                         siT[:, 0:3 * P].rearrange("r (c i) -> r c i", c=3)).then_inc(si_out, 16)
            sp.wait_ge(si_out, 16)
            load_si(0, 0, 0)
            load_si(0, 1, 1)
            sp.wait_ge(si_sb, 2)
            sp.dma_start(si_rows[3], siT[:, 3 * P:4 * P]).then_inc(si_out, 16)
            sp.wait_ge(si_out, 32)
            with sp.Fori(2, UNITS - 1, 2) as u:
                for s in range(2):
                    sp.wait_ge(masks, (u + (s - 1)) * GROUPS)
                    load_si(head_of(u + s), (u + s) % CHUNKS, s)

            def load_x1(f):
                sp.dma_start(yc[:, f % 2], x1_dram[:, 4 * f * D:4 * (f + 1) * D].rearrange("p (t d) -> p t d", t=4)).then_inc(x1_in[f % 2], 16)

            for s in range(2):
                sp.wait_ge(x1_out[s], 16 * (T // 2))
            sp.wait_ge(h_mean_set, 1)
            for f in range(2):
                load_x1(f)
            for f in range(T // 4):
                sp.wait_ge(final, f + 1)
                sp.dma_start(out[:, 4 * f * D:4 * (f + 1) * D].rearrange("p (t d) -> p t d", t=4), yc[:, f % 2]).then_inc(out_done[f % 2], 16)
                if f + 2 < T // 4:
                    sp.wait_ge(out_done[f % 2], 16 * (f // 2 + 1))
                    load_x1(f + 2)
            for s in range(2):
                sp.wait_ge(out_done[s], 16 * (T // 8))

        @block.gpsimd
        def _(pool):
            pool.memset(mean_w, 1.0 / N).then_inc(ones_set, 1)
            pool.memset(cols, 0.0).then_inc(ones_set, 1)
            pool.memset(b_aug[:, D:W0], 0.0).then_inc(ones_set, 1)
            pool.memset(G[:, :, 3 * W0:3 * W0 + 1], 1.0).then_inc(ones_set, 1)
            pool.memset(h_sum[:, :], 0.0)
            pool.wait_ge(hn0, 4)
            pool.memset(hfeat[:, :, :, HD:HW], 1.0).then_inc(ones_set, 1)

            def add_beta(m, s):
                pool.wait_ge(var1, m + 1)
                pool.tensor_tensor(x1_beta[:, s], x_in[:, s], beta_b[:, :], ALU.add).then_inc(x1_plus, 1)

            def add_to_sum(t):
                pool.drain()
                pool.wait_ge(feat, t + 1)
                if isinstance(t, int):
                    src = hfeat[:, t].rearrange("p h w -> p (h w)")
                else:
                    src = hfeat[:, ds(t, 1)].rearrange("p a h w -> p (a h w)")
                pool.tensor_tensor(h_sum[:, :], h_sum[:, :], src, ALU.add).then_inc(h_summed, 1)

            pool.wait_ge(const_late, 16 * LATE_CONSTS)
            for m in range(2):
                add_beta(m, m)
            with pool.Fori(2, T - 1, 2) as m:
                for s in range(2):
                    pool.wait_ge(x1_out[s], m * 8)
                    add_beta(m + s, s)
                    add_to_sum(m + (s - 2))
            for t in range(T - 2, T):
                add_to_sum(t)

        @block.scalar
        def _(act):
            for dst, src in ((ident[:, :], eye[:, :]), (wt_fc, w_fc_t[:, :]), (wdst, w_att[D:2 * D, :]), (w_aug[:, 0:D], w_fc[:, :]),
                             (b_aug[:, 0:D], b_fc[0].partition_broadcast(P))):
                act.dma_start(dst, src).then_inc(const_in, 16)

            def fill_ring(t, s):
                act.wait_ge(compared, t * 4 + 4)
                if not (isinstance(t, int) and t < 2):
                    act.wait_ge(rows_done, t - 1)
                if isinstance(t, int):
                    src = mask[:, t].rearrange("p b c -> p (b c)")
                else:
                    act.nop(nofuse=True)
                    src = mask[:, ds(t, 1)].rearrange("p a b c -> p (a b c)")
                act.activation(ring[:, s].rearrange("p b c -> p (b c)").bitcast(I16), src.bitcast(I16), ACT.Copy).then_inc(in_ring, 1)

            def piece_sqrt(k):
                act.wait_ge(var0, k + 1)
                act.activation(agg0[k][:, 4, :], agg0[k][:, 3, :], ACT.Sqrt).then_inc(sd0, 1)

            piece_sqrt(0)
            piece_sqrt(1)
            for k in range(PIECES):
                for half in range(2):
                    act.wait_ge(t0, 2 * k + half + 1)
                    if k:
                        act.wait_ge(hp0, 2 * k + half - 1)
                    act.activation(hT_all[:, 4 * half:4 * half + 4].rearrange("p t d -> p (t d)"), psT[half],
                                   ACT.Relu).then_inc(hT0, 1)
                if k + 2 < PIECES:
                    piece_sqrt(k + 2)
            fill_ring(0, 0)
            act.wait_ge(mx, 3)
            act.activation(e_w, Hbuf[:, :, D], ACT.Exp, bias=mv[:, 3:4]).then_inc(e0, 1)

            for k in range(5):
                if k < 4:
                    act.wait_ge(g_f32, k + 1)
                    act.activation(G[:, 8 * k:8 * k + 8, 0:W0], Hbuf[:, 8 * k:8 * k + 8], ACT.Copy).then_inc(g_hi, 1)
                if k:
                    act.wait_ge(g_rest, k)
                    act.activation(G[:, 8 * k - 8:8 * k, W0:2 * W0], Hbuf[:, 8 * k - 8:8 * k], ACT.Copy).then_inc(g_mid, 1)

            def cols_of(dram, m):
                return dram[:, m * D:(m + 1) * D] if isinstance(m, int) else dram[:, ds(m * D, D)]

            def store_x1(m, s):
                act.wait_ge(x1_plus, m + 1)
                act.dma_start(cols_of(x1_dram, m), x1_beta[:, s]).then_inc(x1_out[s], 16)

            def tile_step(m, s):
                if not (isinstance(m, int) and m >= T - 2):
                    fill_ring(m + 2, s)
                if not (isinstance(m, int) and m == 0):
                    relu(m - 1, 1 - s)
                act.wait_ge(var1, m + 1)
                act.activation(mv[:, 6:7], mv[:, 5:6], ACT.Sqrt).then_inc(sd1, 1)
                if not (isinstance(m, int) and m == 0):
                    store_x1(m - 1, 1 - s)
                    if not (isinstance(m, int) and m == T - 1):
                        act.dma_start(x_in[:, 1 - s], cols_of(x, m + 1)).then_inc(x_tile[1 - s], 16)
                    features(m - 1, 1 - s)

            def relu(m, s):
                act.wait_ge(t1, m + 1)
                act.activation(hT[:, s], psT[s][:, 0:D], ACT.Relu).then_inc(hT1, 1)

            def features(m, s):
                act.wait_ge(feat_ps, m + 1)
                if isinstance(m, int):
                    dst, d_si, d_sj = hfeat[:, m, :, 0:HD], si[:, m, :], sj[:, m, :]
                else:
                    dst = hfeat[:, ds(m, 1), :, 0:HD].rearrange("p a h w -> p (a h) w")
                    d_si, d_sj = tile_of(si, m), tile_of(sj, m)
                act.activation(d_si, psF[s][:, D:D + H], ACT.Copy)
                act.activation(d_sj, psF[s][:, D + H:D + 2 * H], ACT.Copy)
                act.activation(dst, psF[s][:, 0:D].rearrange("p (h w) -> p h w", h=H), ACT.Copy).then_inc(feat, 1)

            fill_ring(1, 1)
            act.wait_ge(ones_set, 5)
            for m in range(2):
                tile_step(m, m)
            with act.Fori(2, T - 3, 2) as m:
                for s in range(2):
                    tile_step(m + s, s)
            tile_step(T - 2, 0)
            act.wait_ge(si_ps, 1)
            act.activation(siT[:, 0:3 * P], psS[0:CHUNK_TILES * H, 0:3 * P], ACT.Copy).then_inc(si_sb, 1)
            tile_step(T - 1, 1)
            relu(T - 1, 1)
            features(T - 1, 1)
            store_x1(T - 1, 1)

            act.wait_ge(arg1, 1)
            act.activation(bd.rearrange("p t k h -> p (t k h)"), bd.rearrange("p t k h -> p (t k h)"), ACT.Exp).then_inc(bd_ready, 1)
            act.wait_ge(arg1, 2)
            act.activation(AC.rearrange("p k t h -> p (k t h)"), AC.rearrange("p k t h -> p (k t h)"), ACT.Exp).then_inc(bd_ready, 1)
            act.wait_ge(si_ps, 2)
            act.activation(siT[:, 3 * P:4 * P], psS[0:CHUNK_TILES * H, 3 * P:4 * P], ACT.Copy).then_inc(si_sb, 1)

            def evacuate(u, s, k):
                if k == 0:
                    act.wait_ge(group_done, (u + 1) * GROUPS)
                act.wait_ge(turned, u * 4 + (k + 1))
                act.activation(E[0:3 * HW, k % 2], ps[0:3 * HW, 4 * s + k, :], ACT.Copy).then_inc(evacuated, 1)

            def v_high(h, b):
                act.wait_ge(v_f32, h * VBATCHES + (b + 1))
                act.activation(v_part(b, 0), work[:, :], ACT.Copy).then_inc(v_hi, 1)

            def v_middle(h, b):
                act.wait_ge(v_rest, h * VBATCHES + (b + 1))
                act.activation(v_part(b, 1), work[:, :], ACT.Copy).then_inc(v_mid, 1)

            def unit(h, c, hooks):
                u, s = h * CHUNKS + c, c % 2
                act.wait_ge(sib_in[s], h * 32 + 16 * (c // 2 + 1))
                for g in range(GROUPS):
                    for hook in hooks.get(g, ()):
                        hook()
                    if not (isinstance(u, int) and u == 0 and g < NEG_SLOTS):
                        act.wait_ge(group_done, u * GROUPS + (g - NEG_SLOTS + 1))
                        act.nop(nofuse=True)
                    for j in range(GT - 1):
                        t = g * GT + j
                        bias = sj[:, t, h:h + 1] if isinstance(h, int) else sj[:, t, ds(h, 1)]
                        act.activation(neg[:, g % NEG_SLOTS, j].bitcast(I8), sib[:, s].rearrange("p t i -> p (t i)"),
                                       ACT.Sign, bias=bias).then_inc(signs, 1)

            def hooks_of(h, c, v=()):
                hooks = {g: [lambda f=f, hh=hh, b=b: f(hh, b)] for g, f, hh, b in v}
                for k in range(4):
                    hooks.setdefault(4 + k, []).append(lambda k=k: evacuate(h * CHUNKS + (c - 1), (c + 1) % 2, k))
                return hooks

            def final_sqrt(f):
                act.wait_ge(varf, f + 1)
                act.activation(agg[:, 4, 0:4], agg[:, 3, 0:4], ACT.Sqrt).then_inc(sdf, 1)

            act.wait_ge(rows_done, T)
            act.wait_ge(si_out, 32)
            v_high(0, 0)
            v_middle(0, 0)
            first = {b + i: [lambda f=f, b=b: f(0, b // 2 + 1)] for b in (0, 2, 4) for i, f in enumerate((v_high, v_middle))}
            unit(0, 0, {g + 1: f for g, f in first.items()})
            for s in range(2):
                act.wait_ge(x1_out[s], 16 * (T // 2))
            unit(0, 1, hooks_of(0, 1))
            with act.Fori(0, H - 1) as h:
                unit(h, 2, hooks_of(h, 2))
                unit(h, 3, hooks_of(h, 3, [(6, v_high, h + 1, 0), (7, v_middle, h + 1, 0)]))
                unit(h + 1, 0, hooks_of(h + 1, 0, [(2 * b + i - 2, f, h + 1, b) for b in (1, 2, 3)
                                                   for i, f in enumerate((v_high, v_middle))]))
                unit(h + 1, 1, hooks_of(h + 1, 1))
            for c in range(2):
                hooks = hooks_of(H - 1, 2 + c)
                for i in range(2):
                    hooks.setdefault(FINAL_GROUP + i, []).append(lambda f=2 * c + i: final_sqrt(f))
                unit(H - 1, 2 + c, hooks)
            final_sqrt(4)
            final_sqrt(5)
            for k in range(4):
                evacuate(UNITS - 1, 1, k)
            final_sqrt(6)
            final_sqrt(7)

        @block.tensor
        def _(pe):
            def mean_of(m):
                pe.wait_ge(hbuf, m + 1)
                pe.matmul(psS, mean_w, Hbuf[:, 4 * m:4 * m + 4, 0:D], start=(m == 0), stop=(m == 7)).then_inc(mean0, 1)

            pe.wait_ge(const_in, 16 * CONSTS)
            pe.matmul(psM[:, 0:1], wt_fc, wdst, start=True, stop=True).then_inc(waug_ps, 1)
            for k in range(PIECES):
                pe.wait_ge(hn0, k + 1)
                for half in range(2):
                    if k:
                        pe.wait_ge(hT0, 2 * k + half - 1)
                    for i in range(4):
                        ins = pe.transpose(psT[half][:, i * P:(i + 1) * P], hn_all[:, 4 * half + i], ident[:, :])
                    ins.then_inc(t0, 1)
                if k == 0:
                    pe.wait_ge(waug, 1)
                for half in range(2):
                    pe.wait_ge(hT0, 2 * k + half + 1)
                    if k:
                        pe.wait_ge(hbuf, 2 * k + half - 1)
                    for i in range(4):
                        ins = pe.matmul(ps[:, h_banks[half] + i // 2, i % 2 * W0:(i % 2 + 1) * W0], hT_all[:, 4 * half + i],
                                        w_aug, start=True, stop=True)
                    ins.then_inc(hp0, 1)
                if k:
                    pe.wait_ge(ones_set, 1)
                    for half in range(2):
                        mean_of(2 * k - 2 + half)
            pe.wait_ge(mx, 1)
            pe.transpose(psM[0:1, 0:P], mv[:, 0:1], ident[:, :]).then_inc(mx_ps, 1)
            pe.wait_ge(mx, 2)
            pe.matmul(psM[:, P:P + 1], mean_w[0:1, :], mv[0:1, 2:3], start=True, stop=True).then_inc(mx_ps, 1)
            for half in range(2):
                mean_of(2 * PIECES - 2 + half)
            pe.wait_ge(const_late, 16 * LATE_CONSTS)
            pe.wait_ge(mx, 3)
            pe.matmul(psM[:, 8:8 + 2 * H], wt_1, cols, start=True, stop=True).then_inc(w1aug_ps, 1)

            def rows(t, s, post):
                pe.wait_ge(in_ring, t + 1)
                if not (isinstance(t, int) and t < 2):
                    pe.wait_ge(rows_read, t - 1)
                pe.nop(nofuse=True)
                for j in range(T):
                    if isinstance(t, int) and t == 0 and j % 8 == 0:
                        pe.wait_ge(g_ready, j // 8 + 1)
                        pe.nop(nofuse=True)
                    ins = pe.matmul(acc[s][:, 0:G_COLS], ring[:, s, j].bitcast(FP8), G[:, j, :],
                                    start=(j == 0), stop=(j == T - 1))
                    if j == 8 and post is not None:
                        turn(post, s)
                    if j == 24 and post is not None:
                        features(post, s)
                        pe.nop(nofuse=True)
                ins.then_inc(rows_done, 1)

            def turn(m, s):
                pe.wait_ge(hn1, m + 1)
                pe.transpose(psT[s][:, 0:D], hn[:, s], ident[:, :]).then_inc(t1, 1)

            def features(m, s):
                pe.wait_ge(hT1, m + 1)
                pe.matmul(psF[s][:, 0:D + 2 * H], hT[:, s], w1_aug, start=True, stop=True).then_inc(feat_ps, 1)

            def turn_si(c):
                return pe.transpose(psS[0:CHUNK_TILES * H, c * P:(c + 1) * P],
                                    si[:, c * CHUNK_TILES:(c + 1) * CHUNK_TILES, :].rearrange("p t h -> p (t h)"), ident[:, :])

            pe.wait_ge(hbuf, 2 * PIECES)
            rows(0, 0, None)
            rows(1, 1, None)
            pe.wait_ge(w1aug, 1)
            with pe.Fori(2, T - 1, 2) as t:
                for s in range(2):
                    rows(t + s, s, t + (s - 2))
            pe.wait_ge(feat, 3 * CHUNK_TILES)
            for c in range(3):
                ins = turn_si(c)
            ins.then_inc(si_ps, 1)
            for s in range(2):
                turn(T - 2 + s, s)
                features(T - 2 + s, s)
            pe.wait_ge(mx1, 1)
            pe.transpose(psM[0:H, 0:P], mv[:, 0:H], ident[:, :]).then_inc(mx1_ps, 1)
            pe.wait_ge(mx1, 2)
            pe.matmul(psM[:, P:P + H], mean_w[0:H, :], mv[0:H, 8:8 + H], start=True, stop=True).then_inc(mx1_ps, 1)
            turn_si(3).then_inc(si_ps, 1)

            def turn_bank(u, s, k):
                pe.wait_ge(evacuated, u * 4 + (k + 1))
                for i in range(4):
                    ins = pe.transpose(ps[:, 4 * s + k, i * 3 * HW:(i + 1) * 3 * HW],
                                       E[0:3 * HW, k % 2, i * P:(i + 1) * P], ident[0:3 * HW, 0:3 * HW])
                ins.then_inc(turned, 1)

            def unit(u, s, hooks):
                h = head_of(u)
                if not (isinstance(u, int) and u == 0):
                    pe.wait_ge(reduced, u * 4 - 3)
                for g in range(GROUPS):
                    pe.wait_ge(masks, u * GROUPS + (g + 1))
                    if g % 2 == 0:
                        pe.wait_ge(v_ready, h * VBATCHES + (g // 2 + 1))
                    pe.nop(nofuse=True)
                    for j in range(GT):
                        t = g * GT + j
                        for k, m in enumerate((pos[:, g % POS_SLOTS, j], neg[:, g % NEG_SLOTS, j])):
                            for half in range(2):
                                ins = pe.matmul(ps[0:3 * HW, 4 * s + 2 * k + half, :], V[:, t, k, :],
                                                m[:, half * 512:(half + 1) * 512].bitcast(FP8),
                                                start=(t == 0), stop=(t == T - 1))
                    ins.then_inc(group_done, 1)
                    for hook in hooks.get(g, ()):
                        hook()

            def turns(u, s):
                return {1 + k: [lambda k=k: turn_bank(u, s, k)] for k in range(4)}

            def mean_of_h():
                pe.wait_ge(h_summed, T)
                pe.matmul(ps[:, 4, 0:H * HW], mean_w, h_sum[:, :], start=True, stop=True).then_inc(h_mean_ps, 1)

            pe.wait_ge(arg1, 1)
            pe.wait_ge(si_sb, 2)
            pe.sem_inc(turned, 2)
            unit(0, 0, {GROUPS - 2: [mean_of_h]})
            pe.wait_ge(h_mean_set, 1)
            with pe.Fori(1, UNITS - 2, 2) as u:
                unit(u, 1, turns(u - 1, 0))
                unit(u + 1, 0, turns(u, 1))
            unit(UNITS - 1, 1, turns(UNITS - 2, 0))
            for k in range(4):
                turn_bank(UNITS - 1, 1, k)

        @block.vector
        def _(dve):
            def row_stats(stats, agg, n):
                m_even, m_odd = stats[:, 0:n, 1], stats[:, 0:n, 4]
                dve.drain()
                dve.tensor_tensor(agg[:, 0, 0:n], m_even, m_odd, ALU.add)
                dve.tensor_tensor(agg[:, 1, 0:n], m_even, m_odd, ALU.subtract)
                dve.tensor_tensor(agg[:, 2, 0:n], stats[:, 0:n, 2], stats[:, 0:n, 5], ALU.add)
                dve.drain()
                dve.tensor_tensor(agg[:, 1, 0:n], agg[:, 1, 0:n], agg[:, 1, 0:n], ALU.mult)
                dve.tensor_scalar(agg[:, 0, 0:n], agg[:, 0, 0:n], 0.5, None, ALU.mult)
                dve.drain()
                dve.scalar_tensor_tensor(agg[:, 2, 0:n], agg[:, 1, 0:n], D / 4.0, agg[:, 2, 0:n], ALU.mult, ALU.add)
                dve.drain()
                return dve.tensor_scalar(agg[:, 3, 0:n], agg[:, 2, 0:n], 1.0 / D, EPS, ALU.mult, ALU.add)

            def compare_quarter(t, q):
                dve.wait_ge(adj_in[q], t * 16 + 16)
                if isinstance(t, int):
                    dst = mask[:, t, 8 * q:8 * q + 8].rearrange("p a b -> p (a b)")
                else:
                    dst = mask[:, ds(t, 1), 8 * q:8 * q + 8].rearrange("p t a b -> p (t a b)")
                dve.tensor_scalar(dst.bitcast(I8), stage[:, q, :], 0.0, float(ONE_FP8), ALU.is_gt, ALU.mult).then_inc(compared, 1)

            def piece_stats(k):
                dve.wait_ge(x_piece[k], 16)
                for i in range(PIECE):
                    dve.bn_stats(stats0[:, i, :], x_all[:, PIECE * k + i, :])
                row_stats(stats0, agg0[k], PIECE).then_inc(var0, 1)
                dve.drain()

            def piece_norm(k):
                dve.wait_ge(sd0, k + 1)
                dve.reciprocal(agg0[k][:, 5, :], agg0[k][:, 4, :])
                dve.drain()
                if k:
                    dve.wait_ge(t0, 2 * k)
                for i in range(PIECE):
                    ins = dve.tensor_scalar(hn_all[:, i], x_all[:, PIECE * k + i, :], agg0[k][:, 0, i:i + 1],
                                            agg0[k][:, 5, i:i + 1], ALU.subtract, ALU.mult)
                ins.then_inc(hn0, 1)

            def piece_out(k):
                for half in range(2):
                    dve.wait_ge(hp0, 2 * k + half + 1)
                    t = PIECE * k + 4 * half
                    dve.tensor_tensor(Hbuf[:, t:t + 4].rearrange("p (c t) d -> p c t d", c=2),
                                      ps[:, h_banks[half]:h_banks[half] + 2, 0:2 * W0].rearrange("p c (t d) -> p c t d", t=2),
                                      b_aug.unsqueeze(1).unsqueeze(1).to_broadcast([P, 2, 2, W0]), ALU.add).then_inc(hbuf, 1)

            def compare(t):
                for q in range(QUARTERS):
                    compare_quarter(t, q)

            piece_stats(0)
            piece_stats(1)
            piece_norm(0)
            dve.wait_ge(waug_ps, 1)
            dve.tensor_copy(w_aug[:, D:W0], psM[:, 0:1]).then_inc(waug, 1)
            piece_stats(2)
            piece_norm(1)
            compare(0)
            dve.wait_ge(ones_set, 3)
            piece_out(0)
            piece_stats(3)
            piece_norm(2)
            piece_out(1)
            piece_norm(3)
            compare(1)
            piece_out(2)
            piece_out(3)
            dve.drain()
            dve.reduce_max(mv[:, 0:1], Hbuf[:, :, D], X_AXIS).then_inc(mx, 1)
            compare_quarter(2, 0)
            dve.wait_ge(mx_ps, 1)
            dve.reduce_max(mv[0:1, 1:2], psM[0:1, 0:P], X_AXIS)
            dve.drain()
            dve.tensor_scalar(mv[0:1, 2:3], mv[0:1, 1:2], float(N), None, ALU.mult).then_inc(mx, 1)
            compare_quarter(2, 1)
            dve.wait_ge(mx_ps, 2)
            dve.tensor_scalar(mv[:, 3:4], psM[:, P:P + 1], -1.0, EXP_SHIFT, ALU.mult, ALU.add).then_inc(mx, 1)
            compare_quarter(2, 2)
            dve.wait_ge(ones_set, 4)
            for step in range(6):
                if step < 4:
                    g = Hbuf[:, 8 * step:8 * step + 8]
                    e = e_w[:, 8 * step:8 * step + 8].unsqueeze(2)
                    dve.wait_ge(e0, 1)
                    dve.wait_ge(mean0, 2 * step + 2)
                    dve.tensor_copy(g[:, :, D:W0], e)
                    dve.tensor_tensor(g[:, :, 0:D], g[:, :, 0:D], e.to_broadcast([P, 8, D]), ALU.mult).then_inc(g_f32, 1)
                if 1 <= step < 5:
                    g = Hbuf[:, 8 * step - 8:8 * step]
                    dve.wait_ge(g_hi, step)
                    dve.tensor_tensor(g, g, G[:, 8 * step - 8:8 * step, 0:W0], ALU.subtract).then_inc(g_rest, 1)
                if step >= 2:
                    dve.wait_ge(g_mid, step - 1)
                    dve.tensor_tensor(G[:, 8 * step - 16:8 * step - 8, 2 * W0:3 * W0], Hbuf[:, 8 * step - 16:8 * step - 8],
                                      G[:, 8 * step - 16:8 * step - 8, W0:2 * W0], ALU.subtract).then_inc(g_ready, 1)
            dve.wait_ge(mean0, 8)
            dve.wait_ge(w1aug_ps, 1)
            dve.tensor_copy(w1_aug[:, D:D + 2 * H], psM[:, 8:8 + 2 * H]).then_inc(w1aug, 1)
            dve.tensor_reduce(h_mean0, psS.rearrange("p (t d) -> p d t", t=4), X_AXIS, ALU.add)

            def rows_out(m, s, n_in, between):
                e_m = empty[:, m:m + 1] if isinstance(m, int) else empty[:, ds(m, 1)]
                between(0)
                dve.wait_ge(rows_done, m + 1)
                dve.tensor_reduce(num, acc[s][:, 0:3 * W0].rearrange("p (k c) -> p c k", k=3), X_AXIS, ALU.add)
                dve.tensor_scalar(e_m, acc[s][:, 3 * W0:3 * W0 + 1], 0.5, None, ALU.is_lt).then_inc(rows_read, 1)
                between(1)
                dve.wait_ge(rows_read, m + 1)
                dve.tensor_tensor(mv[:, 0:1], num[:, D:W0], e_m, ALU.add)
                dve.scalar_tensor_tensor(num[:, 0:D], h_mean0, e_m, num[:, 0:D], ALU.mult, ALU.add).then_inc(num_set, 1)
                between(2)
                dve.wait_ge(num_set, m + 1)
                dve.reciprocal(mv[:, 1:2], mv[:, 0:1])
                dve.drain()
                dve.wait_ge(x_tile[s], n_in)
                dve.scalar_tensor_tensor(x_in[:, s], num[:, 0:D], mv[:, 1:2], x_in[:, s], ALU.mult, ALU.add)
                dve.drain()
                dve.bn_stats(stats[:, 0, :], x_in[:, s])
                dve.drain()
                dve.bn_aggr(mv[:, 2:4], stats[:, 0, :])
                dve.drain()
                dve.tensor_scalar(mv[:, 5:6], mv[:, 3:4], EPS, None, ALU.add).then_inc(var1, 1)
                between(3)
                dve.wait_ge(sd1, m + 1)
                dve.reciprocal(mv[:, 4:5], mv[:, 6:7])
                dve.drain()
                dve.tensor_scalar(hn[:, s], x_in[:, s], mv[:, 2:3], mv[:, 4:5], ALU.subtract, ALU.mult).then_inc(hn1, 1)

            compare_quarter(2, 3)
            compare(LEAD - 1)
            with dve.Fori(0, T - LEAD - 1, 2) as m:
                for s in range(2):
                    rows_out(m + s, s, m * 8 + 16, lambda q: compare_quarter(m + (s + LEAD), q))
            for m in range(T - LEAD, T):
                rows_out(m, m % 2, 16 * (m // 2 + 1), lambda q: None)

            dve.wait_ge(feat, T)
            dve.drain()
            dve.tensor_reduce(mv[:, 0:H], sj[:, :, :].rearrange("p t h -> p h t"), X_AXIS, ALU.max).then_inc(mx1, 1)
            dve.wait_ge(mx1_ps, 1)
            dve.reduce_max(mv[0:H, 4:5], psM[0:H, 0:P], X_AXIS)
            dve.drain()
            dve.tensor_scalar(mv[0:H, 8:8 + H], ident[0:H, 0:H], mv[0:H, 4:5], float(N), ALU.mult, ALU.mult).then_inc(mx1, 1)
            dve.wait_ge(mx1_ps, 2)
            sj_max = psM[:, P:P + H].unsqueeze(1).to_broadcast([P, T, H])
            dve.tensor_tensor(bd[:, :, 0, :], sj[:, :, :], sj_max, ALU.subtract)
            dve.tensor_tensor(AC[:, 0], si[:, :, :], sj_max, ALU.add)
            dve.drain()
            dve.tensor_scalar(bd[:, :, 1, :], bd[:, :, 0, :], ALPHA, EXP_SHIFT, ALU.mult, ALU.add)
            dve.drain()
            dve.tensor_scalar(bd[:, :, 0, :], bd[:, :, 0, :], EXP_SHIFT, None, ALU.add).then_inc(arg1, 1)
            dve.tensor_scalar(AC[:, 1], AC[:, 0], ALPHA - 1.0, 0.0, ALU.mult, ALU.min)
            dve.drain()
            dve.tensor_scalar(AC[:, 0], AC[:, 0], 1.0 - ALPHA, 0.0, ALU.mult, ALU.min).then_inc(arg1, 1)
            dve.tensor_scalar(nsj, sj[:, :, :], -1.0, None, ALU.mult)
            dve.drain()

            def v_weighted(h, b):
                t = b * VB
                if not (isinstance(h, int) and h == 0):
                    dve.wait_ge(group_done, h * (CHUNKS * GROUPS) + (2 * b + 2 - GROUPS))
                if not (isinstance(h, int) and h == 0 and b == 0):
                    dve.wait_ge(v_ready, h * VBATCHES + b)
                if isinstance(h, int):
                    src = hfeat[:, t:t + VB, h, :]
                    w = [bd[:, t:t + VB, k, h:h + 1] for k in range(2)]
                else:
                    src = hfeat[:, t:t + VB, ds(h, 1), :].rearrange("p t a w -> p t (a w)")
                    w = [bd[:, t:t + VB, k, ds(h, 1)] for k in range(2)]
                for k in range(2):
                    ins = dve.tensor_tensor(work[:, k], src, w[k].to_broadcast([P, VB, HW]), ALU.mult)
                ins.then_inc(v_f32, 1)

            def v_remainder(h, b):
                dve.wait_ge(v_hi, h * VBATCHES + (b + 1))
                dve.tensor_tensor(work[:, :], work[:, :], v_part(b, 0), ALU.subtract).then_inc(v_rest, 1)

            def v_low(h, b):
                dve.wait_ge(v_mid, h * VBATCHES + (b + 1))
                dve.tensor_tensor(v_part(b, 2), work[:, :], v_part(b, 1), ALU.subtract).then_inc(v_ready, 1)

            def reduce_bank(u, s, k):
                dve.wait_ge(turned, u * 4 + (k + 3))
                if k == 0 and not (isinstance(u, int) and u == 0):
                    dve.wait_ge(combine_step, u * COMBINE_STEPS)
                dve.tensor_reduce(R[:, k // 2, 4 * (k % 2):4 * (k % 2) + 4],
                                  ps[:, 4 * s + k, 0:4 * 3 * HW].rearrange("p (t k c) -> p t c k", t=4, k=3),
                                  X_AXIS, ALU.add).then_inc(reduced, 1)

            def combine(h, c, step):
                u = h * CHUNKS + c
                rows = slice(c * CHUNK_TILES, (c + 1) * CHUNK_TILES)
                hs = slice(h, h + 1) if isinstance(h, int) else ds(h, 1)
                shape = [P, CHUNK_TILES, HD]
                if step:
                    dve.wait_ge(combine_step, u * COMBINE_STEPS + step)
                if step == 0:
                    dve.wait_ge(reduced, u * 4 + 5)
                    for k in range(2):
                        ins = dve.tensor_tensor(R[:, k], R[:, k], AC[:, k, rows, hs].to_broadcast([P, CHUNK_TILES, HW]), ALU.mult)
                elif step == 1:
                    ins = dve.tensor_tensor(R[:, 0], R[:, 0], R[:, 1], ALU.add)
                elif step == 2:
                    mean = h_sum[:, h * HW:h * HW + HD] if isinstance(h, int) else h_sum[:, ds(h * HW, HD)]
                    dve.tensor_tensor(R[:, 1, :, 0:HD], mean.unsqueeze(1).to_broadcast(shape),
                                      empty[:, rows].unsqueeze(2).to_broadcast(shape), ALU.mult)
                    ins = dve.tensor_tensor(rden[:, 0, :], R[:, 0, :, HD], empty[:, rows], ALU.add)
                elif step == 3:
                    dve.tensor_tensor(R[:, 0, :, 0:HD], R[:, 0, :, 0:HD], R[:, 1, :, 0:HD], ALU.add)
                    ins = dve.reciprocal(rden[:, 2, :], rden[:, 0, :])
                else:
                    dst = hfeat[:, rows, hs, 0:HD].rearrange("p t a w -> p t (a w)")
                    ins = dve.tensor_tensor(dst, R[:, 0, :, 0:HD], rden[:, 2, :].unsqueeze(2).to_broadcast(shape), ALU.mult)
                ins.then_inc(combine_step, 1)

            def unit(h, c, hooks):
                u, s = h * CHUNKS + c, c % 2
                first = isinstance(u, int) and u == 0
                dve.wait_ge(sib_in[s], h * 32 + 16 * (c // 2 + 1))

                def sign(g):
                    if not (first and g < NEG_SLOTS):
                        dve.wait_ge(group_done, u * GROUPS + (g - NEG_SLOTS + 1))
                    t = g * GT + GT - 1
                    bias = nsj[:, t, h:h + 1] if isinstance(h, int) else nsj[:, t, ds(h, 1)]
                    dve.tensor_scalar(neg[:, g % NEG_SLOTS, GT - 1].bitcast(I8), sib[:, s].rearrange("p t i -> p (t i)"),
                                      bias, -1.0, ALU.is_lt, ALU.mult).then_inc(own_signs, 1)

                sign(0)
                for g in range(GROUPS):
                    for hook in hooks.get(g, ()):
                        hook()
                    m = mask[:, c * CHUNK_TILES:(c + 1) * CHUNK_TILES, g * GT:(g + 1) * GT, :]
                    m = m.bitcast(U32).rearrange("p i j n -> p j i n")
                    nv = neg[:, g % NEG_SLOTS].bitcast(U32).rearrange("p j (i n) -> p j i n", i=CHUNK_TILES)
                    pv = pos[:, g % POS_SLOTS].bitcast(U32).rearrange("p j (i n) -> p j i n", i=CHUNK_TILES)
                    dve.wait_ge(signs, (u * GROUPS + (g + 1)) * (GT - 1))
                    dve.wait_ge(own_signs, u * GROUPS + (g + 1))
                    dve.tensor_tensor(nv, nv, m, ALU.bitwise_and).then_inc(negs, 1)
                    if g + 1 < GROUPS:
                        sign(g + 1)
                    dve.wait_ge(negs, u * GROUPS + (g + 1))
                    if not (first and g < POS_SLOTS):
                        dve.wait_ge(group_done, u * GROUPS + (g - POS_SLOTS + 1))
                    dve.tensor_tensor(pv, nv, m, ALU.bitwise_xor).then_inc(masks, 1)
                for hook in hooks.get(GROUPS, ()):
                    hook()

            def before(h, c, n):
                return (h, c - n) if c >= n else (h - 1, c - n + CHUNKS)

            def hooks_of(h, c, v=()):
                hooks = {}
                if not (isinstance(h, int) and h * CHUNKS + c < 2):
                    hb, cb = before(h, c, 2)
                    for step in range(COMBINE_STEPS):
                        hooks.setdefault(step, []).append(lambda step=step: combine(hb, cb, step))
                for g, f, hh, b in v:
                    hooks.setdefault(g, []).append(lambda f=f, hh=hh, b=b: f(hh, b))
                for k in range(4):
                    hooks.setdefault(5 + k, []).append(lambda k=k: reduce_bank(h * CHUNKS + (c - 1), (c + 1) % 2, k))
                return hooks

            def final_rows(f):
                o = hfeat[:, 4 * f:4 * f + 4, :, 0:HD]
                y = yc[:, f % 2].rearrange("p t (h w) -> p t h w", h=H)
                dve.wait_ge(combine_step, (UNITS - CHUNKS + f // 2 + 1) * COMBINE_STEPS)
                if f:
                    dve.wait_ge(final, f)
                for i in range(4):
                    dve.bn_stats(stats[:, i, :], o[:, i])
                row_stats(stats, agg, 4).then_inc(varf, 1)
                gamma_h = gamma_b[:, :].rearrange("p (h w) -> p h w", h=H)
                for i in range(4):
                    dve.scalar_tensor_tensor(o[:, i], o[:, i], agg[:, 0, i:i + 1], gamma_h, ALU.subtract, ALU.mult)
                dve.wait_ge(sdf, f + 1)
                dve.reciprocal(agg[:, 5, 0:4], agg[:, 4, 0:4])
                dve.drain()
                dve.wait_ge(x1_in[f % 2], 16 * (f // 2 + 1))
                for i in range(4):
                    ins = dve.scalar_tensor_tensor(y[:, i], o[:, i], agg[:, 5, i:i + 1], y[:, i], ALU.mult, ALU.add)
                ins.then_inc(final, 1)

            def set_h_mean():
                dve.wait_ge(h_mean_ps, 1)
                dve.tensor_copy(h_sum[:, :], ps[:, 4, 0:H * HW]).then_inc(h_mean_set, 1)

            dve.sem_inc(reduced, 1)
            dve.wait_ge(rows_done, T)
            dve.wait_ge(bd_ready, 1)
            for step in (v_weighted, v_remainder, v_low):
                step(0, 0)
            steps = [(2 * b - 2 + i, f, 0, b) for b in (1, 2, 3) for i, f in enumerate((v_weighted, v_remainder, v_low))]
            unit(0, 0, {g: [lambda f=f, b=b: f(0, b) for gg, f, _, b in steps if gg == g] for g in range(GROUPS)})
            set_h_mean()
            for s in range(2):
                dve.wait_ge(x1_out[s], 16 * (T // 2))
            dve.wait_ge(bd_ready, 2)
            unit(0, 1, hooks_of(0, 1))
            with dve.Fori(0, H - 1) as h:
                unit(h, 2, hooks_of(h, 2))
                unit(h, 3, hooks_of(h, 3, [(4 + i, f, h + 1, 0) for i, f in enumerate((v_weighted, v_remainder, v_low))]
                                    + [(6, v_weighted, h + 1, 1), (7, v_remainder, h + 1, 1)]))
                unit(h + 1, 0, hooks_of(h + 1, 0, [(0, v_low, h + 1, 1)]
                                        + [(2 * b - 4 + i, f, h + 1, b) for b in (2, 3)
                                           for i, f in enumerate((v_weighted, v_remainder, v_low))]))
                unit(h + 1, 1, hooks_of(h + 1, 1))
            for c in range(2):
                hooks = hooks_of(H - 1, 2 + c)
                for i in range(2):
                    hooks.setdefault(FINAL_GROUP + i, []).append(lambda f=2 * c + i: final_rows(f))
                unit(H - 1, 2 + c, hooks)
            for step in range(COMBINE_STEPS):
                combine(H - 1, 2, step)
            final_rows(4)
            final_rows(5)
            for k in range(4):
                reduce_bank(UNITS - 1, 1, k)
            for step in range(COMBINE_STEPS):
                combine(H - 1, 3, step)
            final_rows(6)
            final_rows(7)


def kernel(x, adj, L0_gnn_W_fc, L0_gnn_b_fc, L0_gnn_w_att, L0_gnn_b_att, L1_gnn_W, L1_gnn_a, L1_gnn_gamma, L1_gnn_beta):
    import concourse.bacc as bacc
    from concourse.bass_utils import run_bass_kernel_spmd

    c = np.ascontiguousarray
    adj = np.asarray(adj).reshape(P, T, P, T).transpose(1, 3, 2, 0)
    adj = adj.reshape(T, QUARTERS, T // QUARTERS, P, P).transpose(0, 1, 3, 2, 4)
    ins = {
        "x": c(x).reshape(P, N),
        "adj": c(adj).reshape(T, QUARTERS, P, QCOLS),
        "w_fc": c(L0_gnn_W_fc),
        "w_fc_t": c(np.asarray(L0_gnn_W_fc).T),
        "b_fc": c(L0_gnn_b_fc).reshape(1, D),
        "w_att": c(L0_gnn_w_att).reshape(2 * D, 1),
        "w1": c(L1_gnn_W),
        "w1_t": c(np.asarray(L1_gnn_W).T),
        "a": c(L1_gnn_a),
        "gamma": c(L1_gnn_gamma).reshape(1, D),
        "beta": c(L1_gnn_beta).reshape(1, D),
        "eye": np.eye(P, dtype=np.float32),
    }
    nc = bacc.Bacc("TRN2", target_bir_lowering=False, num_devices=1)
    aps = [nc.dram_tensor(f"in_{k}", v.shape, mybir.dt.from_np(v.dtype), kind="ExternalInput").ap() for k, v in ins.items()]
    si_rows = nc.dram_tensor("si_rows", (CHUNKS, CHUNK_TILES * H, P), F32, kind="Internal").ap()
    x1_dram = nc.dram_tensor("x1_rows", (P, N), F32, kind="Internal").ap()
    out = nc.dram_tensor("out_rows", (P, N), F32, kind="ExternalOutput").ap()
    build(nc, *aps, si_rows, x1_dram, out)
    r = run_bass_kernel_spmd(nc, [{f"in_{k}": v for k, v in ins.items()}], core_ids=[0])
    return r.results[0]["out_rows"].reshape(N, D)
```

```python
import numpy as np
from contextlib import ExitStack
import concourse.bass as bass
from concourse import mybir

ALU = mybir.AluOpType
ACT = mybir.ActivationFunctionType
X_AXIS = mybir.AxisListType.X
F32, BF16, FP8 = mybir.dt.float32, mybir.dt.bfloat16, mybir.dt.float8e4
I32, U32, I16, I8, U8 = mybir.dt.int32, mybir.dt.uint32, mybir.dt.int16, mybir.dt.int8, mybir.dt.uint8
ds = bass.ds

P = 128
N = 4096
T = N // P
D = 128
H = 4
HD = D // H
HW = HD + 1
ALPHA = 0.2
EPS = 1e-5
EXP_SHIFT = 60.0
ONE_FP8 = 0x38

W0 = D + 1
G_COLS = 3 * W0 + 1
QUARTERS = 4
QCOLS = T // QUARTERS * P

CHUNK_TILES = 8
CHUNKS = T // CHUNK_TILES
CH = CHUNK_TILES * P
UNITS = H * CHUNKS
GT = 4
GROUPS = T // GT
NEG_SLOTS = 4
POS_SLOTS = 2
VB = 8
VBATCHES = T // VB
RAW_TILES = 5
LEAD = 5
SKIPS = (8, 18)
PIECE = 8
PIECES = T // PIECE
FINAL_GROUP = 6
COMBINE_STEPS = 5
ARENA = 57376


class Arena:

    def __init__(self, memory, size):
        self.memory, self.size, self.at = memory, size, 0

    def take(self, count, dt, width):
        start, self.at = self.at, self.at + count * width
        assert self.at <= self.size, self.at
        return self.memory[:, start:self.at].bitcast(dt)


def build(nc, x, adj, w_fc, w_fc_t, b_fc, w_att, w1, w1_t, a, gamma, beta, eye, si_rows, x1_dram, out):
    with ExitStack() as ctx:
        def sb(name, shape, dt):
            return ctx.enter_context(nc.sbuf_tensor(name, shape, dt))

        def sem(name):
            return ctx.enter_context(nc.semaphore(name))

        mask = sb("mask", [P, T, T, P], U8)
        hfeat = sb("hfeat", [P, T, H, HW], F32)
        arena = sb("arena", [P, ARENA], U8)
        late = sb("late", [P, 2 * 4 * D * 4], U8)
        consts = sb("consts", [P, P + HW], F32)
        ident, add_parts = consts[:, 0:P], consts[0:3 * HW, P:P + HW]
        gamma_b = sb("gamma_b", [P, D], F32)
        beta_b = sb("beta_b", [P, D], F32)
        empty = sb("empty", [P, T], F32)
        sj = sb("sj", [P, T, H], F32)
        h_sum = sb("h_sum", [P, H * HW], F32)
        stats = sb("stats", [P, 8, 6], F32)
        agg = sb("agg", [P, 2, 4, 2], F32)
        std = sb("std", [P, 2, 3, 4], F32)
        mv = sb("mv", [P, 16], F32)
        eps = sb("eps", [P, 1], F32)
        rden = sb("rden", [P, 2, CHUNK_TILES], F32)
        ps = ctx.enter_context(nc.psum_tensor("ps", [P, 8, 512], F32))

        one = Arena(arena[:, :], ARENA)
        ring = one.take(2 * T * P, U8, 1).rearrange("p (s t i) -> p s t i", s=2, t=T)
        stage = one.take(QUARTERS * QCOLS, I32, 4).rearrange("p (q n) -> p q n", q=QUARTERS)
        G = one.take(T * G_COLS, BF16, 2).rearrange("p (t n) -> p t n", t=T)
        x1_beta = one.take(2 * D, F32, 4).rearrange("p (s d) -> p s d", s=2)
        x1 = one.take(2 * D, F32, 4).rearrange("p (s d) -> p s d", s=2)
        hn = one.take(2 * D, F32, 4).rearrange("p (s d) -> p s d", s=2)
        hT = one.take(2 * D, F32, 4).rearrange("p (s d) -> p s d", s=2)
        num = one.take(W0, F32, 4)
        one_row = one.take(H, F32, 4)
        h_mean0 = one.take(D, F32, 4)
        w1_aug = one.take(D + 2 * H, F32, 4)

        two = Arena(arena[:, :], ARENA)
        V = two.take(T * 2 * 3 * HW, BF16, 2).rearrange("p (t k n) -> p t k n", t=T, k=2)
        sib = two.take(2 * CH, F32, 4).rearrange("p (s t i) -> p s t i", s=2, t=CHUNK_TILES)
        neg = two.take(NEG_SLOTS * GT * CH, U8, 1).rearrange("p (s t n) -> p s t n", s=NEG_SLOTS, t=GT)
        pos = two.take(POS_SLOTS * GT * CH, U8, 1).rearrange("p (s t n) -> p s t n", s=POS_SLOTS, t=GT)
        E = two.take(2 * 512, F32, 4).rearrange("p (s n) -> p s n", s=2)
        R = two.take(2 * CHUNK_TILES * HW, F32, 4).rearrange("p (k t n) -> p k t n", k=2, t=CHUNK_TILES)
        work = two.take(2 * VB * HW, F32, 4).rearrange("p (k t n) -> p k t n", k=2, t=VB)
        bd = two.take(T * 2 * H, F32, 4).rearrange("p (t k h) -> p t k h", t=T, k=2)
        AC = two.take(2 * T * H, F32, 4).rearrange("p (k t h) -> p k t h", k=2, t=T)
        nsj = two.take(T * H, F32, 4).rearrange("p (t h) -> p t h", t=T)
        siT = two.memory[0:CHUNK_TILES * H, (T - VB) * 2 * 3 * HW * 2:][:, 0:4 * P * 4].bitcast(F32)

        tail = Arena(mask[:, 25:T, :, :].rearrange("p a b c -> p (a b c)"), 7 * T * P)
        hT_all = tail.take(2 * PIECE * D, F32, 4).rearrange("p (s t d) -> p s t d", s=2, t=PIECE)
        hn_all = mask[:, 2:4, :, :].rearrange("p a b c -> p (a b c)").bitcast(F32).rearrange("p (s t d) -> p s t d", s=2, t=PIECE)
        Hbuf = tail.take(T * W0, F32, 4).rearrange("p (t d) -> p t d", t=T)
        wt_fc = tail.take(D, F32, 4)
        wt_1 = tail.take(D, F32, 4)
        b_aug = tail.take(W0, F32, 4)
        cols = tail.take(2 * H, F32, 4)
        wdst = tail.take(1, F32, 4)
        e_w = tail.take(T, F32, 4)
        stats0 = [tail.take(PIECE * 6, F32, 4).rearrange("p (t n) -> p t n", t=PIECE) for _ in range(2)]
        agg0 = [tail.take(2 * PIECE, F32, 4).rearrange("p (t n) -> p t n", n=2) for _ in range(PIECES)]
        std0 = [tail.take(3 * PIECE, F32, 4).rearrange("p (n t) -> p n t", n=3) for _ in range(PIECES)]
        raw = mask[:, 25 - 4 * RAW_TILES:25, :, :].rearrange("p (k a) b c -> p k (a b c)", k=RAW_TILES).bitcast(I32)
        x_all = hfeat[:, :, :, :].rearrange("p t h w -> p (t h w)")[:, T * H:T * H + N].rearrange("p (t d) -> p t d", t=T)

        early = Arena(late[:, :], 2 * 4 * D * 4)
        mean_w = early.take(P, F32, 4)
        w_aug = early.take(W0, F32, 4)
        si = early.take(T * H, F32, 4).rearrange("p (t h) -> p t h", t=T)
        yc = late[:, :].bitcast(F32).rearrange("p (s t d) -> p s t d", s=2, t=4)

        def y_of(f):
            if f < T // 4 - 2:
                return yc[:, f % 2]
            return sib[:, 0].rearrange("p t i -> p (t i)").rearrange("p (s t d) -> p s t d", s=2, t=4)[:, f % 2]

        const_in, const_late = sem("const_in"), sem("const_late")
        ones_set, h_ones = sem("ones_set"), sem("h_ones")
        x_piece = [sem(f"x_piece{k}") for k in range(4)]
        waug_ps, waug, w1aug_ps, w1aug = sem("waug_ps"), sem("waug"), sem("w1aug_ps"), sem("w1aug")
        var0, sd0, scale0, t0, hT0 = sem("var0"), sem("sd0"), sem("scale0"), sem("t0"), sem("hT0")
        hn0 = [sem("hn0_scalar"), sem("hn0_vector")]
        hp0, hbuf, mean0 = sem("hp0"), sem("hbuf"), sem("mean0")
        mx, mx_ps, e0 = sem("mx"), sem("mx_ps"), sem("e0")
        g_f32, g_hi, g_rest, g_mid, g_ready = sem("g_f32"), sem("g_hi"), sem("g_rest"), sem("g_mid"), sem("g_ready")
        adj_in = [sem(f"adj_in{q}") for q in range(QUARTERS)]
        raw_in = [sem(f"raw_in{k}") for k in range(RAW_TILES)]
        compared, raw_compared, in_ring = sem("compared"), sem("raw_compared"), sem("in_ring")
        rows_done, rows_read = sem("rows_done"), sem("rows_read")
        x1_out = [sem(f"x1_out{s}") for s in range(2)]
        x1_plus, num_set = sem("x1_plus"), sem("num_set")
        var1, sd1, hn1, t1, hT1 = sem("var1"), sem("sd1"), sem("hn1"), sem("t1"), sem("hT1")
        feat_ps, feat = sem("feat_ps"), sem("feat")
        si_ps, si_sb, si_out = sem("si_ps"), sem("si_sb"), sem("si_out")
        sib_in = [sem(f"sib_in{s}") for s in range(2)]
        mx1, mx1_ps, arg1, bd_ready = sem("mx1"), sem("mx1_ps"), sem("arg1"), sem("bd_ready")
        v_f32, v_hi, v_rest, v_mid, v_ready = sem("v_f32"), sem("v_hi"), sem("v_rest"), sem("v_mid"), sem("v_ready")
        signs, own_signs, negs, masks, group_done = sem("signs"), sem("own_signs"), sem("negs"), sem("masks"), sem("group_done")
        evacuated, turned, reduced = sem("evacuated"), sem("turned"), sem("reduced")
        h_summed, h_mean_ps, h_mean_set = sem("h_summed"), sem("h_mean_ps"), sem("h_mean_set")
        combine_step = sem("combine_step")
        x1_in = [sem(f"x1_in{s}") for s in range(2)]
        varf, sdf, scalef, normed, final = sem("varf"), sem("sdf"), sem("scalef"), sem("normed"), sem("final")
        out_done = [sem(f"out_done{s}") for s in range(2)]

        acc = [ps[:, 0, :], ps[:, 1, :]]
        psT = [ps[:, 2, :], ps[:, 3, :]]
        psF = [ps[:, 4, :], ps[:, 5, :]]
        psS, psM = ps[:, 6, :], ps[:, 7, :]
        h_banks = [0, 4]
        CONSTS, LATE_CONSTS = 5, 4 + 2 * H
        block = ctx.enter_context(nc.Block())

        def head_of(u):
            return u // CHUNKS if isinstance(u, int) else (u // CHUNKS).with_bounds(max_val=H - 1)

        def summed_on_pe(h, c):
            return c == 2 or (c in (1, 3) and isinstance(h, int) and h == H - 1)

        def tile_of(tensor, t):
            if isinstance(t, int):
                return tensor[:, t]
            v = tensor[:, ds(t, 1)]
            return v.rearrange("p a b -> p (a b)") if len(v.shape) == 3 else v.rearrange("p a b c -> p (a b) c")

        def v_part(b, k):
            return V[:, b * VB:(b + 1) * VB, :, k * HW:(k + 1) * HW].rearrange("p t k n -> p k t n")

        @block.sync
        def _(sp):
            for k in range(4):
                sp.dma_start(x_all[:, 8 * k:8 * k + 8, :],
                             x[:, 8 * k * D:(8 * k + 8) * D].rearrange("p (t d) -> p t d", t=8)).then_inc(x_piece[k], 16)
            for q in range(QUARTERS):
                sp.dma_start(stage[:, q, :], adj[0, q]).then_inc(adj_in[q], 16)
            for dst, src in ((w1_aug[:, 0:D], w1[:, :]), (wt_1, w1_t[:, :]), (gamma_b[:, :], gamma[0].partition_broadcast(P)),
                             (beta_b[:, :], beta[0].partition_broadcast(P))):
                sp.dma_start(dst, src).then_inc(const_late, 16)
            sp.wait_ge(ones_set, 2)
            for h in range(H):
                for k in range(2):
                    sp.dma_start(cols[h * HD:(h + 1) * HD, k * H + h:k * H + h + 1],
                                 a[k * HD:(k + 1) * HD, :]).then_inc(const_late, 16)
            for k in range(RAW_TILES):
                sp.dma_start(raw[:, k].rearrange("p (q n) -> p q n", q=QUARTERS),
                             adj[1 + k].rearrange("q p n -> p q n")).then_inc(raw_in[k], 16)
            with sp.Fori(1 + RAW_TILES, T) as t:
                for q in range(QUARTERS):
                    sp.wait_ge(compared, (t - RAW_TILES) * 4 + (q - 3))
                    sp.dma_start(stage[:, q, :], adj[ds(t, 1), q].rearrange("a p n -> (a p) n")).then_inc(adj_in[q], 16)

            si_by_head = si_rows.rearrange("c (t h) i -> c h t i", h=H)

            def load_si(h, c, s):
                if isinstance(h, int):
                    src = si_by_head[c, h]
                else:
                    src = si_by_head[ds(c, 1), ds(h, 1)].rearrange("a b t i -> (a b t) i")
                sp.dma_start(sib[:, s], src.partition_broadcast(P)).then_inc(sib_in[s], 16)

            sp.wait_ge(compared, 4 * (T - RAW_TILES))
            sp.wait_ge(si_sb, 1)
            sp.dma_start(si_rows[0:3].rearrange("c r i -> r c i"),
                         siT[:, 0:3 * P].rearrange("r (c i) -> r c i", c=3)).then_inc(si_out, 16)
            sp.wait_ge(si_out, 16)
            load_si(0, 0, 0)
            load_si(0, 1, 1)
            sp.wait_ge(si_sb, 2)
            sp.dma_start(si_rows[3], siT[:, 3 * P:4 * P]).then_inc(si_out, 16)
            sp.wait_ge(si_out, 32)
            with sp.Fori(2, UNITS - 1, 2) as u:
                for s in range(2):
                    sp.wait_ge(masks, (u + (s - 1)) * GROUPS)
                    load_si(head_of(u + s), (u + s) % CHUNKS, s)

            def load_x1(f):
                sp.dma_start(y_of(f), x1_dram[:, 4 * f * D:4 * (f + 1) * D].rearrange("p (t d) -> p t d", t=4)).then_inc(x1_in[f % 2], 16)

            for s in range(2):
                sp.wait_ge(x1_out[s], 16 * (T // 2))
            sp.wait_ge(h_mean_set, 1)
            for f in range(2):
                load_x1(f)
            for f in range(T // 4):
                sp.wait_ge(final, f + 1)
                sp.dma_start(out[:, 4 * f * D:4 * (f + 1) * D].rearrange("p (t d) -> p t d", t=4), y_of(f)).then_inc(out_done[f % 2], 16)
                if f + 2 < T // 4 - 2:
                    sp.wait_ge(out_done[f % 2], 16 * (f // 2 + 1))
                    load_x1(f + 2)
                elif f + 2 < T // 4:
                    sp.wait_ge(masks, (UNITS - 1) * GROUPS)
                    sp.wait_ge(x1_in[f % 2], 16 * (f // 2 + 1))
                    load_x1(f + 2)
            for s in range(2):
                sp.wait_ge(out_done[s], 16 * (T // 8))

        @block.gpsimd
        def _(pool):
            pool.memset(eps[:, :], EPS)
            pool.memset(mean_w, 1.0 / N).then_inc(ones_set, 1)
            pool.memset(cols, 0.0).then_inc(ones_set, 1)
            pool.memset(b_aug[:, D:W0], 0.0).then_inc(ones_set, 1)
            pool.memset(G[:, :, 3 * W0:3 * W0 + 1], 1.0).then_inc(ones_set, 1)
            pool.memset(h_sum[:, :], 0.0)
            pool.memset(one_row, 1.0)
            pool.drain()

            def add_beta(m, s):
                pool.wait_ge(var1, m + 1)
                pool.tensor_tensor(x1_beta[:, s], x1[:, s], beta_b[:, :], ALU.add).then_inc(x1_plus, 1)
                ones = hfeat[:, m, :, HD:HW] if isinstance(m, int) else hfeat[:, ds(m, 1), :, HD:HW].rearrange("p a h w -> p (a h) w")
                pool.tensor_tensor(ones, one_row.unsqueeze(2), one_row.unsqueeze(2), ALU.mult).then_inc(h_ones, 1)

            def add_to_sum(t):
                pool.drain()
                pool.wait_ge(feat, t + 1)
                if isinstance(t, int):
                    src = hfeat[:, t].rearrange("p h w -> p (h w)")
                else:
                    src = hfeat[:, ds(t, 1)].rearrange("p a h w -> p (a h w)")
                pool.tensor_tensor(h_sum[:, :], h_sum[:, :], src, ALU.add).then_inc(h_summed, 1)

            pool.wait_ge(const_late, 16 * LATE_CONSTS)
            for m in range(2):
                add_beta(m, m)
            with pool.Fori(2, T - 1, 2) as m:
                for s in range(2):
                    pool.wait_ge(x1_out[s], m * 8)
                    add_beta(m + s, s)
                    add_to_sum(m + (s - 2))
            for t in range(T - 2, T):
                add_to_sum(t)

        @block.scalar
        def _(act):
            for dst, src in ((consts[:, :], eye[:, :]), (wt_fc, w_fc_t[:, :]), (wdst, w_att[D:2 * D, :]), (w_aug[:, 0:D], w_fc[:, :]),
                             (b_aug[:, 0:D], b_fc[0].partition_broadcast(P))):
                act.dma_start(dst, src).then_inc(const_in, 16)

            def fill_ring(t, s):
                if isinstance(t, int) and 1 <= t <= RAW_TILES:
                    act.wait_ge(raw_compared, 4 * t)
                elif isinstance(t, int) and t == 0:
                    act.wait_ge(compared, 4)
                else:
                    act.wait_ge(compared, (t - RAW_TILES) * 4 + 4)
                if not (isinstance(t, int) and t < 2):
                    act.wait_ge(rows_done, t - 1)
                if isinstance(t, int):
                    src = mask[:, t].rearrange("p b c -> p (b c)")
                else:
                    act.nop(nofuse=True)
                    src = mask[:, ds(t, 1)].rearrange("p a b c -> p (a b c)")
                act.activation(ring[:, s].rearrange("p b c -> p (b c)").bitcast(I16), src.bitcast(I16), ACT.Copy).then_inc(in_ring, 1)

            def piece_sqrt(k):
                act.wait_ge(var0, k + 1)
                act.activation(std0[k][:, 0, :], agg0[k][:, :, 1], ACT.Sqrt, bias=eps[:, :]).then_inc(sd0, 1)

            def piece_norm(k):
                act.wait_ge(scale0, k + 1)
                if k >= 2:
                    act.wait_ge(t0, 2 * k - 3)
                for i in range(4):
                    ins = act.activation(hn_all[:, k % 2, i], x_all[:, PIECE * k + i, :], ACT.Identity,
                                         bias=std0[k][:, 2, i:i + 1], scale=std0[k][:, 1, i:i + 1])
                ins.then_inc(hn0[0], 1)

            act.wait_ge(ones_set, 1)
            piece_sqrt(0)
            piece_sqrt(1)
            piece_norm(0)
            piece_norm(1)
            for k in range(PIECES):
                for half in range(2):
                    act.wait_ge(t0, 2 * k + half + 1)
                    if k >= 2:
                        act.wait_ge(hp0, 2 * k + half - 3)
                    act.activation(hT_all[:, k % 2, 4 * half:4 * half + 4].rearrange("p t d -> p (t d)"), psT[half],
                                   ACT.Relu).then_inc(hT0, 1)
                if k + 2 < PIECES:
                    piece_sqrt(k + 2)
                    piece_norm(k + 2)
            fill_ring(0, 0)
            act.wait_ge(mx, 3)
            act.activation(e_w, Hbuf[:, :, D], ACT.Exp, bias=mv[:, 3:4]).then_inc(e0, 1)

            for k in range(5):
                if k < 4:
                    act.wait_ge(g_f32, k + 1)
                    act.activation(G[:, 8 * k:8 * k + 8, 0:W0], Hbuf[:, 8 * k:8 * k + 8], ACT.Copy).then_inc(g_hi, 1)
                if k:
                    act.wait_ge(g_rest, k)
                    act.activation(G[:, 8 * k - 8:8 * k, W0:2 * W0], Hbuf[:, 8 * k - 8:8 * k], ACT.Copy).then_inc(g_mid, 1)

            def sign(h, c, g, j):
                t = g * GT + j
                bias = sj[:, t, h:h + 1] if isinstance(h, int) else sj[:, t, ds(h, 1)]
                act.activation(neg[:, g % NEG_SLOTS, j].bitcast(I8), sib[:, c % 2].rearrange("p t i -> p (t i)"),
                               ACT.Sign, bias=bias).then_inc(signs, 1)

            def store_x1(m, s):
                act.wait_ge(x1_plus, m + 1)
                dst = x1_dram[:, m * D:(m + 1) * D] if isinstance(m, int) else x1_dram[:, ds(m * D, D)]
                act.dma_start(dst, x1_beta[:, s]).then_inc(x1_out[s], 16)

            def tile_step(m, s):
                if not (isinstance(m, int) and m >= T - 2):
                    fill_ring(m + 2, s)
                if not (isinstance(m, int) and m == 0):
                    relu(m - 1, 1 - s)
                act.wait_ge(var1, m + 1)
                act.activation(mv[:, 6:7], mv[:, 3:4], ACT.Sqrt, bias=eps[:, :]).then_inc(sd1, 1)
                if not (isinstance(m, int) and m == 0):
                    store_x1(m - 1, 1 - s)
                    features(m - 1, 1 - s)

            def relu(m, s):
                act.wait_ge(t1, m + 1)
                act.activation(hT[:, s], psT[s][:, 0:D], ACT.Relu).then_inc(hT1, 1)

            def features(m, s):
                act.wait_ge(feat_ps, m + 1)
                if isinstance(m, int):
                    dst, d_si, d_sj = hfeat[:, m, :, 0:HD], si[:, m, :], sj[:, m, :]
                else:
                    dst = hfeat[:, ds(m, 1), :, 0:HD].rearrange("p a h w -> p (a h) w")
                    d_si, d_sj = tile_of(si, m), tile_of(sj, m)
                act.activation(d_si, psF[s][:, D:D + H], ACT.Copy)
                act.activation(d_sj, psF[s][:, D + H:D + 2 * H], ACT.Copy)
                act.activation(dst, psF[s][:, 0:D].rearrange("p (h w) -> p h w", h=H), ACT.Copy).then_inc(feat, 1)

            fill_ring(1, 1)
            for m in range(RAW_TILES - 1):
                tile_step(m, m % 2)
            with act.Fori(RAW_TILES - 1, T - 5, 2) as m:
                for s in range(2):
                    tile_step(m + s, s)
            tile_step(T - 4, 0)
            act.wait_ge(compared, 4 * (T - RAW_TILES))
            act.wait_ge(si_ps, 1)
            act.activation(siT[:, 0:3 * P], psS[0:CHUNK_TILES * H, 0:3 * P], ACT.Copy).then_inc(si_sb, 1)
            tile_step(T - 3, 1)
            tile_step(T - 2, 0)
            act.wait_ge(sib_in[0], 16)
            sign(0, 0, 0, 0)
            relu(T - 2, 0)
            sign(0, 0, 0, 1)
            features(T - 2, 0)
            act.wait_ge(var1, T)
            act.activation(mv[:, 6:7], mv[:, 3:4], ACT.Sqrt, bias=eps[:, :]).then_inc(sd1, 1)
            store_x1(T - 2, 0)
            relu(T - 1, 1)
            features(T - 1, 1)
            store_x1(T - 1, 1)
            sign(0, 0, 0, 2)

            act.wait_ge(arg1, 1)
            act.activation(bd.rearrange("p t k h -> p (t k h)"), bd.rearrange("p t k h -> p (t k h)"), ACT.Exp).then_inc(bd_ready, 1)
            act.wait_ge(arg1, 2)
            act.activation(AC.rearrange("p k t h -> p (k t h)"), AC.rearrange("p k t h -> p (k t h)"), ACT.Exp).then_inc(bd_ready, 1)
            act.wait_ge(si_ps, 2)
            act.activation(siT[:, 3 * P:4 * P], psS[0:CHUNK_TILES * H, 3 * P:4 * P], ACT.Copy).then_inc(si_sb, 1)

            def evacuate(u, s, k):
                if k == 0:
                    act.wait_ge(group_done, (u + 1) * GROUPS)
                act.wait_ge(turned, u * 4 + (k + 1))
                act.activation(E[0:3 * HW, k % 2], ps[0:3 * HW, 4 * s + k, :], ACT.Copy).then_inc(evacuated, 1)

            def v_high(h, b):
                act.wait_ge(v_f32, h * VBATCHES + (b + 1))
                act.activation(v_part(b, 0), work[:, :], ACT.Copy).then_inc(v_hi, 1)

            def v_middle(h, b):
                act.wait_ge(v_rest, h * VBATCHES + (b + 1))
                act.activation(v_part(b, 1), work[:, :], ACT.Copy).then_inc(v_mid, 1)

            def unit(h, c, hooks):
                u, s = h * CHUNKS + c, c % 2
                act.wait_ge(sib_in[s], h * 32 + 16 * (c // 2 + 1))
                for g in range(GROUPS):
                    for hook in hooks.get(g, ()):
                        hook()
                    if not (isinstance(u, int) and u == 0 and g < NEG_SLOTS):
                        act.wait_ge(group_done, u * GROUPS + (g - NEG_SLOTS + 1))
                        act.nop(nofuse=True)
                    if not (isinstance(u, int) and u == 0 and g < 2):
                        for j in range(GT - 1):
                            sign(h, c, g, j)

            def hooks_of(h, c, v=()):
                hooks = {g: [lambda f=f, hh=hh, b=b: f(hh, b)] for g, f, hh, b in v}
                for k in range(4):
                    hooks.setdefault(4 + k, []).append(lambda k=k: evacuate(h * CHUNKS + (c - 1), (c + 1) % 2, k))
                return hooks

            def final_sqrt(f):
                act.wait_ge(varf, f + 1)
                act.activation(std[:, f % 2, 0, :], agg[:, f % 2, :, 1], ACT.Sqrt, bias=eps[:, :]).then_inc(sdf, 1)

            def final_norm(f):
                act.wait_ge(scalef, f + 1)
                for i in range(4):
                    o = hfeat[:, 4 * f + i, :, 0:HD]
                    ins = act.activation(o, o, ACT.Identity, bias=std[:, f % 2, 2, i:i + 1], scale=std[:, f % 2, 1, i:i + 1])
                ins.then_inc(normed, 1)

            act.wait_ge(rows_done, T)
            v_high(0, 0)
            sign(0, 0, 1, 0)
            v_middle(0, 0)
            sign(0, 0, 1, 1)
            sign(0, 0, 1, 2)
            first = {b + i: [lambda f=f, b=b: f(0, b // 2 + 1)] for b in (0, 2, 4) for i, f in enumerate((v_high, v_middle))}
            first[4].insert(0, lambda: act.wait_ge(si_out, 32))
            unit(0, 0, {g + 1: f for g, f in first.items()})
            for s in range(2):
                act.wait_ge(x1_out[s], 16 * (T // 2))
            unit(0, 1, hooks_of(0, 1))
            with act.Fori(0, H - 1) as h:
                unit(h, 2, hooks_of(h, 2))
                unit(h, 3, hooks_of(h, 3, [(6, v_high, h + 1, 0), (7, v_middle, h + 1, 0)]))
                unit(h + 1, 0, hooks_of(h + 1, 0, [(2 * b + i - 2, f, h + 1, b) for b in (1, 2, 3)
                                                   for i, f in enumerate((v_high, v_middle))]))
                unit(h + 1, 1, hooks_of(h + 1, 1))
            for c in range(2):
                hooks = hooks_of(H - 1, 2 + c)
                for i in range(2):
                    hooks.setdefault(FINAL_GROUP + i, []).append(lambda f=2 * c + i: final_sqrt(f))
                if c:
                    hooks.setdefault(1, []).append(lambda: final_norm(1))
                unit(H - 1, 2 + c, hooks)
                final_norm(2 * c)
            final_norm(3)
            for k in range(4):
                evacuate(UNITS - 1, 1, k)
                if k == 1:
                    final_sqrt(4)
                    final_sqrt(5)
            final_norm(4)
            final_norm(5)
            final_sqrt(6)
            final_sqrt(7)
            final_norm(6)
            final_norm(7)

        @block.tensor
        def _(pe):
            def mean_of(m):
                pe.wait_ge(hbuf, m + 1)
                pe.matmul(psS, mean_w, Hbuf[:, 4 * m:4 * m + 4, 0:D], start=(m == 0), stop=(m == 7)).then_inc(mean0, 1)

            pe.wait_ge(const_in, 16 * CONSTS)
            pe.matmul(psM[:, 0:1], wt_fc, wdst, start=True, stop=True).then_inc(waug_ps, 1)
            def turn_piece(k, half):
                pe.wait_ge(hn0[half], k + 1)
                for i in range(4):
                    ins = pe.transpose(psT[half][:, i * P:(i + 1) * P], hn_all[:, k % 2, 4 * half + i], ident)
                ins.then_inc(t0, 1)

            for half in range(2):
                turn_piece(0, half)
            pe.wait_ge(waug, 1)
            for k in range(PIECES):
                for half in range(2):
                    pe.wait_ge(hT0, 2 * k + half + 1)
                    if k + 1 < PIECES:
                        turn_piece(k + 1, half)
                    if k:
                        pe.wait_ge(hbuf, 2 * k + half - 1)
                    for i in range(4):
                        ins = pe.matmul(ps[:, h_banks[half] + i // 2, i % 2 * W0:(i % 2 + 1) * W0], hT_all[:, k % 2, 4 * half + i],
                                        w_aug, start=True, stop=True)
                    ins.then_inc(hp0, 1)
            pe.wait_ge(ones_set, 2)
            pe.wait_ge(mx, 1)
            pe.transpose(psM[0:1, 0:P], mv[:, 0:1], ident).then_inc(mx_ps, 1)
            pe.wait_ge(mx, 2)
            pe.matmul(psM[:, P:P + 1], mean_w[0:1, :], mv[0:1, 2:3], start=True, stop=True).then_inc(mx_ps, 1)
            for m in range(2 * PIECES):
                mean_of(m)
            pe.wait_ge(const_late, 16 * LATE_CONSTS)
            pe.wait_ge(mx, 3)
            pe.matmul(psM[:, 8:8 + 2 * H], wt_1, cols, start=True, stop=True).then_inc(w1aug_ps, 1)

            def rows(t, s, post):
                pe.wait_ge(in_ring, t + 1)
                if not (isinstance(t, int) and t < 2):
                    pe.wait_ge(rows_read, t - 1)
                pe.nop(nofuse=True)
                for j in range(T):
                    if isinstance(t, int) and t == 0 and j % 8 == 0:
                        pe.wait_ge(g_ready, j // 8 + 1)
                        pe.nop(nofuse=True)
                    ins = pe.matmul(acc[s][:, 0:G_COLS], ring[:, s, j].bitcast(FP8), G[:, j, :],
                                    start=(j == 0), stop=(j == T - 1))
                    if j == 8 and post is not None:
                        turn(post, s)
                    if j == 24 and post is not None:
                        features(post, s)
                        pe.nop(nofuse=True)
                ins.then_inc(rows_done, 1)

            def turn(m, s):
                pe.wait_ge(hn1, m + 1)
                pe.transpose(psT[s][:, 0:D], hn[:, s], ident).then_inc(t1, 1)

            def features(m, s):
                pe.wait_ge(hT1, m + 1)
                pe.matmul(psF[s][:, 0:D + 2 * H], hT[:, s], w1_aug, start=True, stop=True).then_inc(feat_ps, 1)

            def turn_si(c):
                return pe.transpose(psS[0:CHUNK_TILES * H, c * P:(c + 1) * P],
                                    si[:, c * CHUNK_TILES:(c + 1) * CHUNK_TILES, :].rearrange("p t h -> p (t h)"), ident)

            pe.wait_ge(hbuf, 2 * PIECES)
            rows(0, 0, None)
            rows(1, 1, None)
            pe.wait_ge(w1aug, 1)
            with pe.Fori(2, T - 3, 2) as t:
                for s in range(2):
                    rows(t + s, s, t + (s - 2))
            pe.wait_ge(feat, 3 * CHUNK_TILES)
            for c in range(3):
                ins = turn_si(c)
            ins.then_inc(si_ps, 1)
            for s in range(2):
                rows(T - 2 + s, s, T - 4 + s)
            for s in range(2):
                turn(T - 2 + s, s)
                features(T - 2 + s, s)
            pe.wait_ge(mx1, 1)
            pe.transpose(psM[0:H, 0:P], mv[:, 0:H], ident).then_inc(mx1_ps, 1)
            pe.wait_ge(mx1, 2)
            pe.matmul(psM[:, P:P + H], mean_w[0:H, :], mv[0:H, 8:8 + H], start=True, stop=True).then_inc(mx1_ps, 1)
            turn_si(3).then_inc(si_ps, 1)

            def turn_bank(h, c, k):
                u, s = h * CHUNKS + c, c % 2
                pe.wait_ge(evacuated, u * 4 + (k + 1))
                for i in range(4):
                    rows = E[0:3 * HW, k % 2, i * P:(i + 1) * P]
                    if summed_on_pe(h, c):
                        at = (k % 2 * 4 + i) * HW
                        ins = pe.matmul(ps[:, 4 * s + k // 2 * 2, at:at + HW], rows, add_parts, start=True, stop=True)
                    else:
                        ins = pe.transpose(ps[:, 4 * s + k, i * 3 * HW:(i + 1) * 3 * HW], rows, ident[0:3 * HW, 0:3 * HW])
                ins.then_inc(turned, 1)

            def unit(h, c, hooks):
                u, s = h * CHUNKS + c, c % 2
                if not (isinstance(u, int) and u == 0):
                    pe.wait_ge(reduced, u * 4 - 3)
                for g in range(GROUPS):
                    pe.wait_ge(masks, u * GROUPS + (g + 1))
                    if g % 2 == 0:
                        pe.wait_ge(v_ready, h * VBATCHES + (g // 2 + 1))
                    pe.nop(nofuse=True)
                    for j in range(GT):
                        t = g * GT + j
                        for k, m in enumerate((pos[:, g % POS_SLOTS, j], neg[:, g % NEG_SLOTS, j])):
                            for half in range(2):
                                ins = pe.matmul(ps[0:3 * HW, 4 * s + 2 * k + half, :], V[:, t, k, :],
                                                m[:, half * 512:(half + 1) * 512].bitcast(FP8),
                                                start=(t == 0), stop=(t == T - 1))
                    ins.then_inc(group_done, 1)
                    for hook in hooks.get(g, ()):
                        hook()

            def turns(h, c):
                return {1 + k: [lambda k=k: turn_bank(h, c, k)] for k in range(4)}

            def mean_of_h():
                pe.wait_ge(h_summed, T)
                pe.matmul(ps[:, 4, 0:H * HW], mean_w, h_sum[:, :], start=True, stop=True).then_inc(h_mean_ps, 1)

            pe.wait_ge(arg1, 1)
            pe.wait_ge(si_sb, 2)
            pe.sem_inc(turned, 2)
            mean_of_h()
            unit(0, 0, {})
            pe.wait_ge(h_mean_set, 1)
            unit(0, 1, turns(0, 0))
            with pe.Fori(0, H - 1) as h:
                unit(h, 2, turns(h, 1))
                unit(h, 3, turns(h, 2))
                unit(h + 1, 0, turns(h, 3))
                unit(h + 1, 1, turns(h + 1, 0))
            unit(H - 1, 2, turns(H - 1, 1))
            unit(H - 1, 3, turns(H - 1, 2))
            for k in range(4):
                turn_bank(H - 1, 3, k)

        @block.vector
        def _(dve):
            def compare_quarter(t, q):
                dve.wait_ge(adj_in[q], 16 if isinstance(t, int) and t == 0 else (t - RAW_TILES) * 16 + 16)
                if isinstance(t, int):
                    dst = mask[:, t, 8 * q:8 * q + 8].rearrange("p a b -> p (a b)")
                else:
                    dst = mask[:, ds(t, 1), 8 * q:8 * q + 8].rearrange("p t a b -> p (t a b)")
                dve.tensor_scalar(dst.bitcast(I8), stage[:, q, :], 0.0, float(ONE_FP8), ALU.is_gt, ALU.mult).then_inc(compared, 1)

            def compare_raw(t, q):
                dve.wait_ge(raw_in[t - 1], 16)
                dve.tensor_scalar(mask[:, t, 8 * q:8 * q + 8].rearrange("p a b -> p (a b)").bitcast(I8),
                                  raw[:, t - 1, q * QCOLS:(q + 1) * QCOLS], 0.0, float(ONE_FP8),
                                  ALU.is_gt, ALU.mult).then_inc(raw_compared, 1)

            def piece_stats(k):
                dve.wait_ge(x_piece[k], 16)
                for i in range(PIECE):
                    dve.bn_stats(stats0[k % 2][:, i, :], x_all[:, PIECE * k + i, :])
                dve.drain()
                for i in range(PIECE):
                    ins = dve.bn_aggr(agg0[k][:, i, :], stats0[k % 2][:, i, :])
                ins.then_inc(var0, 1)

            def piece_scale(k):
                mean, inverse = agg0[k][:, :, 0], std0[k][:, 1, :]
                dve.wait_ge(sd0, k + 1)
                dve.reciprocal(inverse, std0[k][:, 0, :])
                dve.drain()
                dve.scalar_tensor_tensor(std0[k][:, 2, 0:4], mean[:, 0:4], -1.0, inverse[:, 0:4], ALU.mult, ALU.mult).then_inc(scale0, 1)
                if k >= 2:
                    dve.wait_ge(t0, 2 * k - 2)
                for i in range(4, PIECE):
                    ins = dve.tensor_scalar(hn_all[:, k % 2, i], x_all[:, PIECE * k + i, :], mean[:, i:i + 1], inverse[:, i:i + 1],
                                            ALU.subtract, ALU.mult)
                ins.then_inc(hn0[1], 1)

            def piece_out(k):
                for half in range(2):
                    dve.wait_ge(hp0, 2 * k + half + 1)
                    t = PIECE * k + 4 * half
                    dve.tensor_tensor(Hbuf[:, t:t + 4].rearrange("p (c t) d -> p c t d", c=2),
                                      ps[:, h_banks[half]:h_banks[half] + 2, 0:2 * W0].rearrange("p c (t d) -> p c t d", t=2),
                                      b_aug.unsqueeze(1).unsqueeze(1).to_broadcast([P, 2, 2, W0]), ALU.add).then_inc(hbuf, 1)

            def compare(t):
                for q in range(QUARTERS):
                    compare_quarter(t, q)

            piece_stats(0)
            piece_stats(1)
            piece_scale(0)
            dve.wait_ge(waug_ps, 1)
            dve.tensor_copy(w_aug[:, D:W0], psM[:, 0:1]).then_inc(waug, 1)
            piece_scale(1)
            piece_stats(2)
            piece_stats(3)
            dve.wait_ge(ones_set, 4)
            piece_scale(2)
            compare_quarter(0, 0)
            piece_out(0)
            compare_quarter(0, 1)
            piece_scale(3)
            compare_quarter(0, 2)
            piece_out(1)
            compare_quarter(0, 3)
            compare_raw(1, 0)
            piece_out(2)
            compare_raw(1, 1)
            piece_out(3)
            dve.drain()
            dve.reduce_max(mv[:, 0:1], Hbuf[:, :, D], X_AXIS).then_inc(mx, 1)
            dve.wait_ge(mx_ps, 1)
            dve.reduce_max(mv[0:1, 1:2], psM[0:1, 0:P], X_AXIS)
            dve.drain()
            dve.tensor_scalar(mv[0:1, 2:3], mv[0:1, 1:2], float(N), None, ALU.mult).then_inc(mx, 1)
            compare_raw(1, 2)
            dve.wait_ge(mx_ps, 2)
            dve.tensor_scalar(mv[:, 3:4], psM[:, P:P + 1], -1.0, EXP_SHIFT, ALU.mult, ALU.add).then_inc(mx, 1)
            compare_raw(1, 3)
            dve.wait_ge(ones_set, 4)
            for step in range(6):
                if step < 4:
                    g = Hbuf[:, 8 * step:8 * step + 8]
                    e = e_w[:, 8 * step:8 * step + 8].unsqueeze(2)
                    dve.wait_ge(e0, 1)
                    dve.wait_ge(mean0, 2 * step + 2)
                    dve.tensor_copy(g[:, :, D:W0], e)
                    dve.tensor_tensor(g[:, :, 0:D], g[:, :, 0:D], e.to_broadcast([P, 8, D]), ALU.mult).then_inc(g_f32, 1)
                if 1 <= step < 5:
                    g = Hbuf[:, 8 * step - 8:8 * step]
                    dve.wait_ge(g_hi, step)
                    dve.tensor_tensor(g, g, G[:, 8 * step - 8:8 * step, 0:W0], ALU.subtract).then_inc(g_rest, 1)
                if step >= 2:
                    dve.wait_ge(g_mid, step - 1)
                    dve.tensor_tensor(G[:, 8 * step - 16:8 * step - 8, 2 * W0:3 * W0], Hbuf[:, 8 * step - 16:8 * step - 8],
                                      G[:, 8 * step - 16:8 * step - 8, W0:2 * W0], ALU.subtract).then_inc(g_ready, 1)
            dve.wait_ge(mean0, 8)
            dve.wait_ge(w1aug_ps, 1)
            dve.tensor_copy(w1_aug[:, D:D + 2 * H], psM[:, 8:8 + 2 * H]).then_inc(w1aug, 1)
            dve.tensor_reduce(h_mean0, psS.rearrange("p (t d) -> p d t", t=4), X_AXIS, ALU.add)

            def rows_out(m, s, between):
                e_m = empty[:, m:m + 1] if isinstance(m, int) else empty[:, ds(m, 1)]
                between(0)
                dve.wait_ge(rows_done, m + 1)
                dve.tensor_reduce(num, acc[s][:, 0:3 * W0].rearrange("p (k c) -> p c k", k=3), X_AXIS, ALU.add)
                dve.tensor_scalar(e_m, acc[s][:, 3 * W0:3 * W0 + 1], 0.5, None, ALU.is_lt).then_inc(rows_read, 1)
                between(1)
                dve.wait_ge(rows_read, m + 1)
                dve.tensor_tensor(mv[:, 0:1], num[:, D:W0], e_m, ALU.add)
                dve.scalar_tensor_tensor(num[:, 0:D], h_mean0, e_m, num[:, 0:D], ALU.mult, ALU.add).then_inc(num_set, 1)
                between(2)
                dve.wait_ge(num_set, m + 1)
                dve.reciprocal(mv[:, 1:2], mv[:, 0:1])
                dve.drain()
                if not (isinstance(m, int) and m < 2):
                    dve.wait_ge(x1_plus, m - 1)
                dve.scalar_tensor_tensor(x1[:, s], num[:, 0:D], mv[:, 1:2], tile_of(x_all, m), ALU.mult, ALU.add)
                dve.drain()
                dve.bn_stats(stats[:, 0, :], x1[:, s])
                dve.drain()
                dve.bn_aggr(mv[:, 2:4], stats[:, 0, :]).then_inc(var1, 1)
                between(3)
                dve.wait_ge(sd1, m + 1)
                dve.reciprocal(mv[:, 4:5], mv[:, 6:7])
                dve.drain()
                dve.tensor_scalar(hn[:, s], x1[:, s], mv[:, 2:3], mv[:, 4:5], ALU.subtract, ALU.mult).then_inc(hn1, 1)

            for q in range(QUARTERS):
                compare_raw(2, q)

            def stage_work(t):
                return [lambda q=q: compare_quarter(t, q) for q in range(QUARTERS)]

            def raw_work(t):
                return [lambda q=q: compare_raw(t, q) for q in range(QUARTERS)]

            def parts(work):
                return lambda i: [f() for f in work[len(work) * i // 4:len(work) * (i + 1) // 4]]

            first = [raw_work(3) + stage_work(6)[0:2], stage_work(6)[2:4] + raw_work(4), raw_work(5) + stage_work(7), stage_work(8)]
            for m in range(4):
                rows_out(m, m % 2, parts(first[m]))
            at, lead = 4, LEAD
            for until in SKIPS:
                with dve.Fori(at, until - 1, 2) as m:
                    for s in range(2):
                        rows_out(m + s, s, parts(stage_work(m + (s + lead))))
                lead -= 1
                rows_out(until, 0, parts([]))
                rows_out(until + 1, 1, parts(stage_work(until + 1 + lead)))
                at = until + 2
            last = (T - lead) // 2 * 2
            with dve.Fori(at, last - 1, 2) as m:
                for s in range(2):
                    rows_out(m + s, s, parts(stage_work(m + (s + lead))))
            for m in range(last, T):
                rows_out(m, m % 2, parts(stage_work(m + lead) if m + lead < T else []))

            def sign(h, c, g):
                u = h * CHUNKS + c
                if not (isinstance(u, int) and u == 0 and g < NEG_SLOTS):
                    dve.wait_ge(group_done, u * GROUPS + (g - NEG_SLOTS + 1))
                t = g * GT + GT - 1
                bias = nsj[:, t, h:h + 1] if isinstance(h, int) else nsj[:, t, ds(h, 1)]
                dve.tensor_scalar(neg[:, g % NEG_SLOTS, GT - 1].bitcast(I8), sib[:, c % 2].rearrange("p t i -> p (t i)"),
                                  bias, -1.0, ALU.is_lt, ALU.mult).then_inc(own_signs, 1)

            dve.wait_ge(h_ones, T)
            dve.wait_ge(feat, T)
            dve.drain()
            dve.tensor_reduce(mv[:, 0:H], sj[:, :, :].rearrange("p t h -> p h t"), X_AXIS, ALU.max).then_inc(mx1, 1)
            dve.tensor_scalar(nsj, sj[:, :, :], -1.0, None, ALU.mult)
            dve.wait_ge(mx1_ps, 1)
            dve.reduce_max(mv[0:H, 4:5], psM[0:H, 0:P], X_AXIS)
            dve.drain()
            dve.tensor_scalar(mv[0:H, 8:8 + H], ident[0:H, 0:H], mv[0:H, 4:5], float(N), ALU.mult, ALU.mult).then_inc(mx1, 1)
            dve.drain()
            dve.wait_ge(sib_in[0], 16)
            sign(0, 0, 0)
            dve.wait_ge(mx1_ps, 2)
            sj_max = psM[:, P:P + H].unsqueeze(1).to_broadcast([P, T, H])
            dve.tensor_tensor(bd[:, :, 0, :], sj[:, :, :], sj_max, ALU.subtract)
            dve.tensor_tensor(AC[:, 0], si[:, :, :], sj_max, ALU.add)
            dve.drain()
            dve.tensor_scalar(bd[:, :, 1, :], bd[:, :, 0, :], ALPHA, EXP_SHIFT, ALU.mult, ALU.add)
            dve.drain()
            dve.tensor_scalar(bd[:, :, 0, :], bd[:, :, 0, :], EXP_SHIFT, None, ALU.add).then_inc(arg1, 1)
            dve.tensor_scalar(AC[:, 1], AC[:, 0], ALPHA - 1.0, 0.0, ALU.mult, ALU.min)
            dve.drain()
            dve.tensor_scalar(AC[:, 0], AC[:, 0], 1.0 - ALPHA, 0.0, ALU.mult, ALU.min).then_inc(arg1, 1)
            def v_weighted(h, b):
                t = b * VB
                if not (isinstance(h, int) and h == 0):
                    dve.wait_ge(group_done, h * (CHUNKS * GROUPS) + (2 * b + 2 - GROUPS))
                if not (isinstance(h, int) and h == 0 and b == 0):
                    dve.wait_ge(v_ready, h * VBATCHES + b)
                if isinstance(h, int):
                    src = hfeat[:, t:t + VB, h, :]
                    w = [bd[:, t:t + VB, k, h:h + 1] for k in range(2)]
                else:
                    src = hfeat[:, t:t + VB, ds(h, 1), :].rearrange("p t a w -> p t (a w)")
                    w = [bd[:, t:t + VB, k, ds(h, 1)] for k in range(2)]
                for k in range(2):
                    ins = dve.tensor_tensor(work[:, k], src, w[k].to_broadcast([P, VB, HW]), ALU.mult)
                ins.then_inc(v_f32, 1)

            def v_remainder(h, b):
                dve.wait_ge(v_hi, h * VBATCHES + (b + 1))
                dve.tensor_tensor(work[:, :], work[:, :], v_part(b, 0), ALU.subtract).then_inc(v_rest, 1)

            def v_low(h, b):
                dve.wait_ge(v_mid, h * VBATCHES + (b + 1))
                dve.tensor_tensor(v_part(b, 2), work[:, :], v_part(b, 1), ALU.subtract).then_inc(v_ready, 1)

            def reduce_bank(h, c, k):
                u, s = h * CHUNKS + c, c % 2
                if summed_on_pe(h, c) and k % 2 == 0:
                    return
                dve.wait_ge(turned, u * 4 + (k + 3))
                if k < 2 and not (isinstance(u, int) and u == 0):
                    dve.wait_ge(combine_step, u * COMBINE_STEPS)
                if summed_on_pe(h, c):
                    rows = slice(c * CHUNK_TILES, (c + 1) * CHUNK_TILES)
                    hs = slice(h, h + 1) if isinstance(h, int) else ds(h, 1)
                    sums = ps[:, 4 * s + k - 1, 0:CHUNK_TILES * HW].rearrange("p (t c) -> p t c", t=CHUNK_TILES)
                    dve.tensor_tensor(R[:, k // 2], sums, AC[:, k // 2, rows, hs].to_broadcast([P, CHUNK_TILES, HW]),
                                      ALU.mult).then_inc(reduced, 2)
                else:
                    dve.tensor_reduce(R[:, k // 2, 4 * (k % 2):4 * (k % 2) + 4],
                                      ps[:, 4 * s + k, 0:4 * 3 * HW].rearrange("p (t k c) -> p t c k", t=4, k=3),
                                      X_AXIS, ALU.add).then_inc(reduced, 1)

            def combine(h, c, step):
                u = h * CHUNKS + c
                rows = slice(c * CHUNK_TILES, (c + 1) * CHUNK_TILES)
                hs = slice(h, h + 1) if isinstance(h, int) else ds(h, 1)
                shape = [P, CHUNK_TILES, HD]
                if step:
                    dve.wait_ge(combine_step, u * COMBINE_STEPS + step)
                else:
                    dve.wait_ge(reduced, u * 4 + 5)
                if step == 0 and summed_on_pe(h, c):
                    dve.sem_inc(combine_step, 1)
                elif step == 0:
                    for k in range(2):
                        ins = dve.tensor_tensor(R[:, k], R[:, k], AC[:, k, rows, hs].to_broadcast([P, CHUNK_TILES, HW]), ALU.mult)
                elif step == 1:
                    ins = dve.tensor_tensor(R[:, 0], R[:, 0], R[:, 1], ALU.add)
                elif step == 2:
                    mean = h_sum[:, h * HW:h * HW + HD] if isinstance(h, int) else h_sum[:, ds(h * HW, HD)]
                    dve.tensor_tensor(R[:, 1, :, 0:HD], mean.unsqueeze(1).to_broadcast(shape),
                                      empty[:, rows].unsqueeze(2).to_broadcast(shape), ALU.mult)
                    ins = dve.tensor_tensor(rden[:, 0, :], R[:, 0, :, HD], empty[:, rows], ALU.add)
                elif step == 3:
                    dve.tensor_tensor(R[:, 0, :, 0:HD], R[:, 0, :, 0:HD], R[:, 1, :, 0:HD], ALU.add)
                    ins = dve.reciprocal(rden[:, 1, :], rden[:, 0, :])
                else:
                    dst = hfeat[:, rows, hs, 0:HD].rearrange("p t a w -> p t (a w)")
                    ins = dve.tensor_tensor(dst, R[:, 0, :, 0:HD], rden[:, 1, :].unsqueeze(2).to_broadcast(shape), ALU.mult)
                if not (step == 0 and summed_on_pe(h, c)):
                    ins.then_inc(combine_step, 1)

            def unit(h, c, hooks):
                u, s = h * CHUNKS + c, c % 2
                first = isinstance(u, int) and u == 0
                dve.wait_ge(sib_in[s], h * 32 + 16 * (c // 2 + 1))
                if not first:
                    sign(h, c, 0)
                for g in range(GROUPS):
                    for hook in hooks.get(g, ()):
                        hook()
                    m = mask[:, c * CHUNK_TILES:(c + 1) * CHUNK_TILES, g * GT:(g + 1) * GT, :]
                    m = m.bitcast(U32).rearrange("p i j n -> p j i n")
                    nv = neg[:, g % NEG_SLOTS].bitcast(U32).rearrange("p j (i n) -> p j i n", i=CHUNK_TILES)
                    pv = pos[:, g % POS_SLOTS].bitcast(U32).rearrange("p j (i n) -> p j i n", i=CHUNK_TILES)
                    dve.wait_ge(signs, (u * GROUPS + (g + 1)) * (GT - 1))
                    dve.wait_ge(own_signs, u * GROUPS + (g + 1))
                    dve.tensor_tensor(nv, nv, m, ALU.bitwise_and).then_inc(negs, 1)
                    if first and g == 0:
                        v_remainder(0, 0)
                    elif g + 1 < GROUPS:
                        sign(h, c, g + 1)
                    dve.wait_ge(negs, u * GROUPS + (g + 1))
                    if not (first and g < POS_SLOTS):
                        dve.wait_ge(group_done, u * GROUPS + (g - POS_SLOTS + 1))
                    dve.tensor_tensor(pv, nv, m, ALU.bitwise_xor).then_inc(masks, 1)
                    if first and g == 0:
                        v_low(0, 0)
                        sign(h, c, 1)
                        v_weighted(0, 1)
                        set_h_mean()
                for hook in hooks.get(GROUPS, ()):
                    hook()

            def before(h, c, n):
                return (h, c - n) if c >= n else (h - 1, c - n + CHUNKS)

            def hooks_of(h, c, v=()):
                hooks = {}
                if not (isinstance(h, int) and h * CHUNKS + c < 2):
                    hb, cb = before(h, c, 2)
                    for step in range(COMBINE_STEPS):
                        hooks.setdefault(step, []).append(lambda step=step: combine(hb, cb, step))
                for g, f, hh, b in v:
                    hooks.setdefault(g, []).append(lambda f=f, hh=hh, b=b: f(hh, b))
                for k in range(4):
                    hooks.setdefault(5 + k, []).append(lambda k=k: reduce_bank(*before(h, c, 1), k))
                return hooks

            def final_stats(f):
                dve.wait_ge(combine_step, (UNITS - CHUNKS + f // 2 + 1) * COMBINE_STEPS)
                for i in range(4):
                    dve.bn_stats(stats[:, 4 * (f % 2) + i, :], hfeat[:, 4 * f + i, :, 0:HD])
                dve.drain()
                for i in range(4):
                    ins = dve.bn_aggr(agg[:, f % 2, i, :], stats[:, 4 * (f % 2) + i, :])
                ins.then_inc(varf, 1)

            def final_scale(f):
                dve.wait_ge(sdf, f + 1)
                dve.reciprocal(std[:, f % 2, 1, :], std[:, f % 2, 0, :])
                dve.drain()
                dve.scalar_tensor_tensor(std[:, f % 2, 2, :], agg[:, f % 2, :, 0], -1.0, std[:, f % 2, 1, :],
                                         ALU.mult, ALU.mult).then_inc(scalef, 1)

            def final_sum(f):
                o = hfeat[:, 4 * f:4 * f + 4, :, 0:HD]
                y = y_of(f).rearrange("p t (h w) -> p t h w", h=H)
                gamma_h = gamma_b[:, :].rearrange("p (h w) -> p h w", h=H).unsqueeze(1).to_broadcast([P, 4, H, HD])
                dve.wait_ge(normed, f + 1)
                dve.tensor_tensor(o, o, gamma_h, ALU.mult)
                dve.drain()
                dve.wait_ge(x1_in[f % 2], 16 * (f // 2 + 1))
                dve.tensor_tensor(y, o, y, ALU.add).then_inc(final, 1)

            def set_h_mean():
                dve.wait_ge(h_mean_ps, 1)
                dve.tensor_copy(h_sum[:, :], ps[:, 4, 0:H * HW]).then_inc(h_mean_set, 1)

            dve.sem_inc(reduced, 1)
            dve.wait_ge(bd_ready, 1)
            v_weighted(0, 0)
            steps = [(2 * b - 2 + i, f, 0, b) for b in (1, 2, 3) for i, f in enumerate((v_weighted, v_remainder, v_low))]
            unit(0, 0, {g: [lambda f=f, b=b: f(0, b) for gg, f, _, b in steps if gg == g] for g in range(1, GROUPS)})
            for s in range(2):
                dve.wait_ge(x1_out[s], 16 * (T // 2))
            dve.wait_ge(bd_ready, 2)
            unit(0, 1, hooks_of(0, 1))
            with dve.Fori(0, H - 1) as h:
                unit(h, 2, hooks_of(h, 2))
                unit(h, 3, hooks_of(h, 3, [(4 + i, f, h + 1, 0) for i, f in enumerate((v_weighted, v_remainder, v_low))]
                                    + [(6, v_weighted, h + 1, 1), (7, v_remainder, h + 1, 1)]))
                unit(h + 1, 0, hooks_of(h + 1, 0, [(0, v_low, h + 1, 1)]
                                        + [(2 * b - 4 + i, f, h + 1, b) for b in (2, 3)
                                           for i, f in enumerate((v_weighted, v_remainder, v_low))]))
                unit(h + 1, 1, hooks_of(h + 1, 1))
            for c in range(2):
                hooks = hooks_of(H - 1, 2 + c)
                for i in range(2):
                    hooks.setdefault(FINAL_GROUP - 1 + i, []).append(lambda f=2 * c + i: final_stats(f))
                    hooks.setdefault(FINAL_GROUP + 1 + i, []).append(lambda f=2 * c + i: final_scale(f))
                    if c:
                        hooks.setdefault(2 + i, []).append(lambda f=i: final_sum(f))
                unit(H - 1, 2 + c, hooks)
            for step in range(COMBINE_STEPS):
                combine(H - 1, 2, step)
            final_sum(2)
            for f in (4, 5):
                final_stats(f)
            final_sum(3)
            reduce_bank(H - 1, 3, 1)
            for f in (4, 5):
                final_scale(f)
            reduce_bank(H - 1, 3, 3)
            for step in range(COMBINE_STEPS):
                combine(H - 1, 3, step)
            final_stats(6)
            final_sum(4)
            final_scale(6)
            final_stats(7)
            final_sum(5)
            final_scale(7)
            for f in (6, 7):
                final_sum(f)


def kernel(x, adj, L0_gnn_W_fc, L0_gnn_b_fc, L0_gnn_w_att, L0_gnn_b_att, L1_gnn_W, L1_gnn_a, L1_gnn_gamma, L1_gnn_beta):
    import concourse.bacc as bacc
    from concourse.bass_utils import run_bass_kernel_spmd

    c = np.ascontiguousarray
    adj = np.asarray(adj).reshape(P, T, P, T).transpose(1, 3, 2, 0)
    adj = adj.reshape(T, QUARTERS, T // QUARTERS, P, P).transpose(0, 1, 3, 2, 4)
    ins = {
        "x": c(x).reshape(P, N),
        "adj": c(adj).reshape(T, QUARTERS, P, QCOLS),
        "w_fc": c(L0_gnn_W_fc),
        "w_fc_t": c(np.asarray(L0_gnn_W_fc).T),
        "b_fc": c(L0_gnn_b_fc).reshape(1, D),
        "w_att": c(L0_gnn_w_att).reshape(2 * D, 1),
        "w1": c(L1_gnn_W),
        "w1_t": c(np.asarray(L1_gnn_W).T),
        "a": c(L1_gnn_a),
        "gamma": c(L1_gnn_gamma).reshape(1, D),
        "beta": c(L1_gnn_beta).reshape(1, D),
        "eye": np.concatenate([np.eye(P), np.eye(HW)[np.arange(P) % HW]], axis=1).astype(np.float32),
    }
    nc = bacc.Bacc("TRN2", target_bir_lowering=False, num_devices=1)
    aps = [nc.dram_tensor(f"in_{k}", v.shape, mybir.dt.from_np(v.dtype), kind="ExternalInput").ap() for k, v in ins.items()]
    si_rows = nc.dram_tensor("si_rows", (CHUNKS, CHUNK_TILES * H, P), F32, kind="Internal").ap()
    x1_dram = nc.dram_tensor("x1_rows", (P, N), F32, kind="Internal").ap()
    out = nc.dram_tensor("out_rows", (P, N), F32, kind="ExternalOutput").ap()
    build(nc, *aps, si_rows, x1_dram, out)
    r = run_bass_kernel_spmd(nc, [{f"in_{k}": v for k, v in ins.items()}], core_ids=[0])
    return r.results[0]["out_rows"].reshape(N, D)
```
